# Optimizing a Trainium2 kernel written in Bass

```python
import numpy as np
import jax
import jax.numpy as jnp

def _softmax(x, axis=-1):
    return jax.nn.softmax(x, axis=axis)

def _gelu(x):
    return jax.nn.gelu(x, approximate=True)

def _silu(x):
    return jax.nn.silu(x)

def _sigmoid(x):
    return jax.nn.sigmoid(x)

def _layernorm(x, axis=-1, eps=1e-05):
    m = jnp.mean(x, axis=axis, keepdims=True)
    v = jnp.var(x, axis=axis, keepdims=True)
    return (x - m) / jnp.sqrt(v + eps)

def _scatter_add(tgt, idx, src, axis=0):
    return tgt.at[idx].add(src)

def _segment_sum(src, seg, n):
    return jax.ops.segment_sum(src, seg, n)
kernel_name = 'mk_seq_preln_d1_jaxref_r8_a7adba'

def setup_inputs(seed: int=0):
    np.random.seed(seed)
    _w = jnp.asarray

    def _L0_attn_setup():
        import jax, jax.numpy as jnp
        import numpy as np
        B, T, H, D, HID, K = (2, 64, 16, 128, 256, 4)
        SCALE = D ** (-0.5)
        LN_EPS = 1e-05

        def _dwconv_causal(x, w, b):
            xt = jnp.transpose(x, (0, 2, 1))
            out = jax.lax.conv_general_dilated(xt, w[:, None, :], window_strides=(1,), padding=[(K - 1, 0)], feature_group_count=w.shape[0])
            return jnp.transpose(out, (0, 2, 1)) + b

        def _delta_scan(q, k, v, a, beta):
            ks = k * SCALE
            xs = tuple((jnp.moveaxis(z, 1, 0) for z in (q, ks, v, a, beta)))

            def step(S, t):
                q_t, k_t, v_t, a_t, b_t = t
                y = jnp.einsum('bhvk,bhk->bhv', S, k_t)
                err = y - v_t
                S = a_t[..., None] * S - (b_t[..., None] * err)[..., None] * k_t[:, :, None, :]
                o = jnp.einsum('bhvk,bhk->bhv', S, q_t)
                return (S, o)
            S0 = jnp.zeros((q.shape[0], H, D, D), q.dtype)
            _, o = jax.lax.scan(step, S0, xs)
            return jnp.moveaxis(o, 0, 1)
        key = jax.random.key(seed)
        ks = jax.random.split(key, 16)
        p = lambda k, shape, s=0.02: jax.random.normal(k, shape, jnp.float32) * s
        return {'x': jax.random.normal(ks[0], (B, T, HID), jnp.float32), 'Wq': p(ks[1], (HID, H * D)), 'Wk': p(ks[2], (HID, H * D)), 'Wv': p(ks[3], (HID, H * D)), 'Wa': p(ks[4], (HID, H * D)), 'ba': jnp.zeros((H * D,), jnp.float32), 'Wb': p(ks[5], (HID, H)), 'bb': jnp.zeros((H,), jnp.float32), 'Wg': p(ks[6], (HID, H * D)), 'Wo': p(ks[7], (H * D, HID)), 'qconv_w': p(ks[8], (H * D, K), 0.2), 'qconv_b': jnp.zeros((H * D,), jnp.float32), 'kconv_w': p(ks[9], (H * D, K), 0.2), 'kconv_b': jnp.zeros((H * D,), jnp.float32), 'vconv_w': p(ks[10], (H * D, K), 0.2), 'vconv_b': jnp.zeros((H * D,), jnp.float32), 'ln_g': jnp.ones((D,), jnp.float32), 'ln_b': jnp.zeros((D,), jnp.float32)}
    _L0_attn_in = _L0_attn_setup()

    def _L0_ffn_setup():
        import jax, jax.numpy as jnp
        import numpy as np
        TOPK = 2
        N_EXPERTS = 8
        ROUTE_SCALE = 1.0
        key = jax.random.key(seed)
        ks = jax.random.split(key, 7)
        B, T, C = (4, 256, 256)
        H = 176
        HS = 352
        E = N_EXPERTS
        s = 0.02
        return {'x': jax.random.normal(ks[0], (B, T, C), jnp.float32), 'gate_w': jax.random.normal(ks[1], (E, C), jnp.float32) * s, 'gate_bias': jnp.zeros((E,), jnp.float32), 'shared_gw': jax.random.normal(ks[2], (2 * HS, C), jnp.float32) * s, 'shared_dw': jax.random.normal(ks[3], (C, HS), jnp.float32) * s, 'up_w': jax.random.normal(ks[4], (E, 2 * H, C), jnp.float32) * s, 'down_w': jax.random.normal(ks[5], (E, C, H), jnp.float32) * s}
    _L0_ffn_in = _L0_ffn_setup()
    _d = {'L0_attn_x': _L0_attn_in['x'], 'L0_attn_Wq': _L0_attn_in['Wq'], 'L0_attn_Wk': _L0_attn_in['Wk'], 'L0_attn_Wv': _L0_attn_in['Wv'], 'L0_attn_Wa': _L0_attn_in['Wa'], 'L0_attn_ba': _L0_attn_in['ba'], 'L0_attn_Wb': _L0_attn_in['Wb'], 'L0_attn_bb': _L0_attn_in['bb'], 'L0_attn_Wg': _L0_attn_in['Wg'], 'L0_attn_Wo': _L0_attn_in['Wo'], 'L0_attn_qconv_w': _L0_attn_in['qconv_w'], 'L0_attn_qconv_b': _L0_attn_in['qconv_b'], 'L0_attn_kconv_w': _L0_attn_in['kconv_w'], 'L0_attn_kconv_b': _L0_attn_in['kconv_b'], 'L0_attn_vconv_w': _L0_attn_in['vconv_w'], 'L0_attn_vconv_b': _L0_attn_in['vconv_b'], 'L0_attn_ln_g': _L0_attn_in['ln_g'], 'L0_attn_ln_b': _L0_attn_in['ln_b'], 'L0_ffn_gate_w': _L0_ffn_in['gate_w'], 'L0_ffn_gate_bias': _L0_ffn_in['gate_bias'], 'L0_ffn_shared_gw': _L0_ffn_in['shared_gw'], 'L0_ffn_shared_dw': _L0_ffn_in['shared_dw'], 'L0_ffn_up_w': _L0_ffn_in['up_w'], 'L0_ffn_down_w': _L0_ffn_in['down_w']}
    _x0 = _d['L0_attn_x']
    _d['L0_attn_x'] = jax.random.normal(jax.random.fold_in(jax.random.key(seed), 1), (1, 2048, 256), dtype=_x0.dtype)
    del _x0
    return _d

def reference(L0_attn_x, L0_attn_Wq, L0_attn_Wk, L0_attn_Wv, L0_attn_Wa, L0_attn_ba, L0_attn_Wb, L0_attn_bb, L0_attn_Wg, L0_attn_Wo, L0_attn_qconv_w, L0_attn_qconv_b, L0_attn_kconv_w, L0_attn_kconv_b, L0_attn_vconv_w, L0_attn_vconv_b, L0_attn_ln_g, L0_attn_ln_b, L0_ffn_gate_w, L0_ffn_gate_bias, L0_ffn_shared_gw, L0_ffn_shared_dw, L0_ffn_up_w, L0_ffn_down_w):

    def _L0_attn_ref(x, Wq, Wk, Wv, Wa, ba, Wb, bb, Wg, Wo, qconv_w, qconv_b, kconv_w, kconv_b, vconv_w, vconv_b, ln_g, ln_b):
        import jax, jax.numpy as jnp
        import numpy as np
        B, T, H, D, HID, K = (2, 64, 16, 128, 256, 4)
        SCALE = D ** (-0.5)
        LN_EPS = 1e-05

        def _dwconv_causal(x, w, b):
            xt = jnp.transpose(x, (0, 2, 1))
            out = jax.lax.conv_general_dilated(xt, w[:, None, :], window_strides=(1,), padding=[(K - 1, 0)], feature_group_count=w.shape[0])
            return jnp.transpose(out, (0, 2, 1)) + b

        def _delta_scan(q, k, v, a, beta):
            ks = k * SCALE
            xs = tuple((jnp.moveaxis(z, 1, 0) for z in (q, ks, v, a, beta)))

            def step(S, t):
                q_t, k_t, v_t, a_t, b_t = t
                y = jnp.einsum('bhvk,bhk->bhv', S, k_t)
                err = y - v_t
                S = a_t[..., None] * S - (b_t[..., None] * err)[..., None] * k_t[:, :, None, :]
                o = jnp.einsum('bhvk,bhk->bhv', S, q_t)
                return (S, o)
            S0 = jnp.zeros((q.shape[0], H, D, D), q.dtype)
            _, o = jax.lax.scan(step, S0, xs)
            return jnp.moveaxis(o, 0, 1)
        b, t, _ = x.shape
        q = jax.nn.silu(_dwconv_causal(x @ Wq, qconv_w, qconv_b)).reshape(b, t, H, D)
        k = jax.nn.silu(_dwconv_causal(x @ Wk, kconv_w, kconv_b)).reshape(b, t, H, D)
        v = jax.nn.silu(_dwconv_causal(x @ Wv, vconv_w, vconv_b)).reshape(b, t, H, D)
        a = jax.nn.sigmoid(x @ Wa + ba).reshape(b, t, H, D)
        beta = jax.nn.sigmoid(x @ Wb + bb)
        o = _delta_scan(q, k, v, a, beta)
        mu = jnp.mean(o, axis=-1, keepdims=True)
        var = jnp.mean(jnp.square(o - mu), axis=-1, keepdims=True)
        o = (o - mu) * jax.lax.rsqrt(var + LN_EPS) * ln_g + ln_b
        g = jax.nn.sigmoid(x @ Wg).reshape(b, t, H, D)
        o = (o * g).reshape(b, t, H * D)
        return o @ Wo

    def _L0_ffn_ref(x, gate_w, gate_bias, shared_gw, shared_dw, up_w, down_w):
        import jax, jax.numpy as jnp
        import numpy as np
        TOPK = 2
        N_EXPERTS = 8
        ROUTE_SCALE = 1.0
        B, T, C = x.shape
        xf = x.reshape(-1, C)
        yg = xf @ shared_gw.T
        y, g = jnp.split(yg, 2, axis=-1)
        shared = jax.nn.silu(g) * y @ shared_dw.T
        scores = jax.nn.sigmoid(xf @ gate_w.T)
        _, topk_idx = jax.lax.top_k(scores + gate_bias, TOPK)
        w = jnp.take_along_axis(scores, topk_idx, axis=-1)
        w = w / jnp.sum(w, axis=-1, keepdims=True) * ROUTE_SCALE
        out = jnp.zeros_like(xf)
        for e in range(N_EXPERTS):
            we = jnp.sum(jnp.where(topk_idx == e, w, 0.0), axis=-1)
            gu = xf @ up_w[e].T
            g_e, u_e = jnp.split(gu, 2, axis=-1)
            h = jax.nn.silu(g_e) * u_e
            out = out + h @ down_w[e].T * we[:, None]
        return (shared + out).reshape(B, T, C)
    x = L0_attn_x
    x = x + _L0_attn_ref(_layernorm(x, axis=-1), L0_attn_Wq, L0_attn_Wk, L0_attn_Wv, L0_attn_Wa, L0_attn_ba, L0_attn_Wb, L0_attn_bb, L0_attn_Wg, L0_attn_Wo, L0_attn_qconv_w, L0_attn_qconv_b, L0_attn_kconv_w, L0_attn_kconv_b, L0_attn_vconv_w, L0_attn_vconv_b, L0_attn_ln_g, L0_attn_ln_b)
    x = x + _L0_ffn_ref(_layernorm(x, axis=-1), L0_ffn_gate_w, L0_ffn_gate_bias, L0_ffn_shared_gw, L0_ffn_shared_dw, L0_ffn_up_w, L0_ffn_down_w)
    return x

_drawn_inputs = setup_inputs


def setup_inputs(seed=0):
    import zlib

    import numpy as np

    out = dict(_drawn_inputs(seed))
    spreads = {'L0_attn_ba': (0.0, 0.8),
     'L0_attn_bb': (0.0, 0.8),
     'L0_attn_qconv_b': (0.0, 0.1),
     'L0_attn_kconv_b': (0.0, 0.1),
     'L0_attn_vconv_b': (0.0, 0.1),
     'L0_attn_ln_g': (1.0, 0.6),
     'L0_attn_ln_b': (0.0, 0.1),
     'L0_ffn_gate_bias': (0.0, 0.8)}
    factors = {'L0_attn_Wa': 8.0,
     'L0_attn_Wb': 7.834,
     'L0_attn_Wg': 5.087,
     'L0_ffn_gate_w': 8.0,
     'L0_ffn_shared_gw': 2.861,
     'L0_ffn_shared_dw': 2.866,
     'L0_ffn_up_w': 5.732,
     'L0_ffn_down_w': 5.741}
    for name, (base, spread) in spreads.items():
        noise = np.random.default_rng([zlib.crc32(name.encode()), seed]).standard_normal(out[name].shape)
        drawn = base * np.exp(spread * noise) if base else spread * noise
        out[name] = jnp.asarray(drawn.astype(out[name].dtype))
    for name, factor in factors.items():
        out[name] = (out[name] * factor).astype(out[name].dtype)
    return out
```

```python
import concourse.bass as bass
from concourse import mybir
from contextlib import ExitStack

FP32 = mybir.dt.float32
ALU = mybir.AluOpType
ACT = mybir.ActivationFunctionType
AXIS = mybir.AxisListType

T, HID = 2048, 256
H, D = 16, 128
TAPS = 4
E, TOPK = 8, 2
HE, HS = 176, 352
EPS = 1e-5
SCALE = float(D) ** -0.5
KT = HID // 128
TT = T // 128

TA = 512
NTA = T // TA
HALO = TAPS - 1
NPROJ = 5
Q_, K_, V_, A_, G_ = range(5)
WCOLS = NPROJ * KT * 128
CCOLS = 3 * (TAPS + 1) + 1

C = 64
R = 4
J = C // R
NCH = T // C
HC = H * C
HJ = H * J
LEVELS = [4, 8, 16, 32]
NC5 = R * (R + 1)

TF = 512
NTF = T // TF
HROWS = E * HE + HS
MT = -(-HROWS // 128)
MROWS = [min(128, HROWS - 128 * m) for m in range(MT)]
ET = E * HE // 128


class Count:

    def __init__(self, sem, per, unit=1, ahead=0):
        self.sem, self.per, self.unit, self.ahead = sem, per, unit, ahead

    def at(self, turn, k):
        return turn * (self.per * self.unit) + (self.ahead * self.per + k) * self.unit

    def start(self, eng):
        if self.ahead:
            eng.sem_inc(self.sem, self.ahead * self.per * self.unit)


def normalize_rows(nc, dve, act_wait, done, x, xc, sq, stat, n, base, signal_var):
    mean, ssq, var = stat[:, 0:n], stat[:, n:2 * n], stat[:, 2 * n:3 * n]
    bc = lambda s: s.unsqueeze(2).to_broadcast([128, n, HID])
    nc.vector.tensor_reduce(ssq, x, AXIS.X, ALU.add).then_inc(done, 1)
    dve.wait_ge(done, base + 1)
    nc.vector.tensor_scalar(mean, ssq, 1.0 / HID, None, ALU.mult).then_inc(done, 1)
    dve.wait_ge(done, base + 2)
    nc.vector.tensor_tensor(xc, x, bc(mean), ALU.subtract).then_inc(done, 1)
    dve.wait_ge(done, base + 3)
    nc.vector.tensor_tensor(sq, xc, xc, ALU.mult).then_inc(done, 1)
    dve.wait_ge(done, base + 4)
    nc.vector.tensor_reduce(ssq, sq, AXIS.X, ALU.add).then_inc(done, 1)
    dve.wait_ge(done, base + 5)
    nc.vector.tensor_scalar(var, ssq, 1.0 / HID, None, ALU.mult).then_inc(signal_var, 1)


def project_inputs(nc, ident, x_d, wb_d, bb_d, wpack_d, scr, nbeta_d):
    ctx = ExitStack()
    with ctx:
        sb = lambda name, shape: ctx.enter_context(nc.sbuf_tensor(name, shape, FP32))
        sem = lambda name: ctx.enter_context(nc.semaphore(name))
        x = sb("A_x", [128, TT, HID])
        xc = sb("A_xc", [128, TT, HID])
        xn = sb("A_xn", [128, TT, HID])
        stat = sb("A_stat", [128, 3 * TT])
        std = sb("A_std", [128, 2 * TT])
        eps = sb("A_eps", [128, 1])
        xT = sb("A_xT", [128, KT, HALO + T])
        factors = sb("A_factors", [128, 2])
        wb = sb("A_wb", [128, KT, H])
        bb = sb("A_bb", [H, 1])
        beta = sb("A_beta", [H, T])
        nbeta = sb("A_nbeta", [H, T])
        w = sb("A_w", [128, 2, WCOLS + CCOLS])
        acc = sb("A_acc", [128, 3, 2, TA])
        outs = sb("A_outs", [128, 2, 3, T])
        outag = sb("A_outag", [128, 2, T])
        psY = [ctx.enter_context(nc.psum_tensor(f"A_psY{i}", [128, 2 * 512], FP32)) for i in range(3)]
        psAG = [ctx.enter_context(nc.psum_tensor(f"A_psAG{i}", [128, 512], FP32)) for i in range(2)]
        loaded, const_ld = sem("A_x_loaded"), sem("A_const_loaded")
        ln_step, var_done, std_done, xn_done = sem("A_ln_step"), sem("A_var"), sem("A_std"), sem("A_xn")
        pads, xT_ps, xT_a, xT_v = sem("A_pads"), sem("A_xT_ps"), sem("A_xT_act"), sem("A_xT_dve")
        beta_ps, beta_sb, nbeta_sb, nbeta_st = sem("A_beta_ps"), sem("A_beta"), sem("A_nbeta"), sem("A_nbeta_st")
        TURNS = H // 2
        w_ld = [Count(sem(f"A_w_ld{s}"), 1, 16) for s in range(2)]
        w_used = [Count(sem(f"A_w_used{s}"), 1, 1, 1) for s in range(2)]
        c_used = [Count(sem(f"A_c_used{s}"), 1, 1, 1) for s in range(2)]
        ca_used = [Count(sem(f"A_ca_used{s}"), 1, 1, 1) for s in range(2)]
        y_full = [Count(sem(f"A_y_full{p}"), 2 * NTA) for p in range(3)]
        ag_full = [Count(sem(f"A_ag_full{p}"), 2 * NTA) for p in range(2)]
        ag_free = [Count(sem(f"A_ag_free{p}"), 2 * NTA, 1, 1) for p in range(2)]
        acc_set = [Count(sem(f"A_acc_set{p}"), 2 * NTA) for p in range(3)]
        tap = [Count(sem(f"A_tap{p}"), 2 * NTA * 3, 1, 1) for p in range(3)]
        sig = [Count(sem(f"A_sig{p}"), 2 * NTA) for p in range(3)]
        silu = [Count(sem(f"A_silu{p}"), 2 * NTA, 1, 1) for p in range(3)]
        scaled = [Count(sem(f"A_scaled{p}"), 2, 1, 1) for p in (K_, V_)]
        st_qkv = [Count(sem(f"A_st_qkv{s}"), 3, 16, 1) for s in range(2)]
        st_ag = Count(sem("A_st_ag"), 4, 16, 2)

        block = ctx.enter_context(nc.Block())

        @block.sync
        def _(sp):
            for i in range(4):
                n = TT // 4
                sp.dma_start(x[:, i * n:(i + 1) * n, :],
                             x_d.rearrange("(n p) c -> p n c", p=128)[:, i * n:(i + 1) * n, :]).then_inc(loaded, 16)
            sp.dma_start(wb[:], wb_d.rearrange("(k p) h -> p k h", p=128)).then_inc(const_ld, 16)
            sp.dma_start(bb[:], bb_d.rearrange("(h o) -> h o", o=1)).then_inc(const_ld, 16)
            for c in (st_qkv[0], st_qkv[1], st_ag):
                c.start(sp)
            for s in range(2):
                sp.dma_start(w[:, s, :], wpack_d[s]).then_inc(w_ld[s].sem, 16)
            sp.wait_ge(nbeta_sb, 1)
            sp.dma_start(nbeta_d, nbeta[:]).then_inc(nbeta_st, 16)
            with sp.Fori(0, TURNS) as t:
                for s in range(2):
                    head = scr[:, :, bass.ds(t * 2 + s, 1), :]
                    sp.wait_ge(silu[Q_].sem, silu[Q_].at(t, (s + 1) * NTA))
                    sp.dma_start(head[Q_], outs[:, s, Q_, :].unsqueeze(1)).then_inc(st_qkv[s].sem, 16)
                    sp.wait_ge(scaled[0].sem, scaled[0].at(t, s + 1))
                    sp.dma_start(head[K_], outs[:, s, K_, :].unsqueeze(1)).then_inc(st_qkv[s].sem, 16)
                    sp.wait_ge(scaled[1].sem, scaled[1].at(t, s + 1))
                    sp.dma_start(head[V_], outs[:, s, V_, :].unsqueeze(1)).then_inc(st_qkv[s].sem, 16)
                    for p in range(2):
                        sp.wait_ge(ag_free[p].sem, ag_free[p].at(t, (s + 1) * NTA))
                        sp.dma_start(head[A_ + p], outag[:, p, :].unsqueeze(1)).then_inc(st_ag.sem, 16)
                    sp.wait_ge(w_used[s].sem, w_used[s].at(t, 1))
                    sp.wait_ge(c_used[s].sem, c_used[s].at(t, 1))
                    sp.wait_ge(ca_used[s].sem, ca_used[s].at(t, 1))
                    sp.dma_start(w[:, s, :], wpack_d[bass.ds(t * 2 + (s + 2), 1)].rearrange("o p c -> p (o c)"))\
                      .then_inc(w_ld[s].sem, 16)
            for s in range(2):
                sp.wait_ge(st_qkv[s].sem, st_qkv[s].at(TURNS, 0))
                sp.wait_ge(w_ld[s].sem, w_ld[s].at(TURNS, 1))
            sp.wait_ge(st_ag.sem, st_ag.at(TURNS, 0))
            sp.wait_ge(nbeta_st, 16)

        @block.gpsimd
        def _(pool):
            nc.gpsimd.memset(xT[:, :, 0:HALO], 0.0).then_inc(pads, 1)
            nc.gpsimd.memset(eps[:], EPS).then_inc(pads, 1)
            nc.gpsimd.memset(factors[:, 0:1], SCALE).then_inc(pads, 1)
            nc.gpsimd.memset(factors[:, 1:2], -1.0).then_inc(pads, 1)
            pool.wait_ge(pads, 4)
            for c in (*scaled, *silu):
                c.start(pool)
            with pool.Fori(0, TURNS) as t:
                for s in range(2):
                    for i in range(NTA):
                        n = s * NTA + i
                        for p in range(3):
                            pool.wait_ge(sig[p].sem, sig[p].at(t, n + 1))
                            o = outs[:, s, p, TA * i:TA * (i + 1)]
                            nc.gpsimd.tensor_tensor(o, o, acc[:, p, n % 2, :], ALU.mult).then_inc(silu[p].sem, 1)
                    for i, (p, factor) in enumerate(((K_, SCALE), (V_, -1.0))):
                        pool.wait_ge(silu[p].sem, silu[p].at(t, (s + 1) * NTA))
                        o = outs[:, s, p, :]
                        nc.gpsimd.tensor_tensor(o, o, factors[:, i:i + 1].to_broadcast([128, T]), ALU.mult)\
                          .then_inc(scaled[i].sem, 1)

        @block.vector
        def _(dve):
            dve.wait_ge(loaded, 64)
            normalize_rows(nc, dve, None, ln_step, x[:], xc[:], xn[:], stat, TT, 0, var_done)
            dve.wait_ge(std_done, 1)
            nc.vector.reciprocal(std[:, TT:2 * TT], std[:, 0:TT]).then_inc(ln_step, 1)
            dve.wait_ge(ln_step, 6)
            dve.wait_ge(var_done, 1)
            nc.vector.tensor_tensor(xn[:], xc[:], std[:, TT:2 * TT].unsqueeze(2).to_broadcast([128, TT, HID]),
                                    ALU.mult).then_inc(xn_done, 1)
            for g in range(4):
                dve.wait_ge(xT_ps, 5 + g)
                src = (psY[2][:, 0:512], psY[2][:, 512:1024], psAG[0][:], psAG[1][:])[g]
                nc.vector.tensor_copy(xT[:, 1, HALO + 512 * g:HALO + 512 * (g + 1)], src).then_inc(xT_v, 1)
            for p in range(3):
                tap[p].start(dve)
            c_used[0].start(dve)
            c_used[1].start(dve)
            with dve.Fori(0, TURNS) as t:
                for s in range(2):
                    dve.wait_ge(w_ld[s].sem, w_ld[s].at(t, 1))
                    for i in range(NTA):
                        n = s * NTA + i
                        for k in range(3):
                            for p in range(3):
                                if k == 0:
                                    dve.wait_ge(acc_set[p].sem, acc_set[p].at(t, n + 1))
                                else:
                                    dve.wait_ge(tap[p].sem, tap[p].at(t, 3 * n + k))
                                a = acc[:, p, n % 2, :].rearrange("p (b c) -> p b c", b=2)
                                j = TAPS - 2 - k
                                y = psY[p][:, :].rearrange("p (b c) -> p b c", b=2)[:, :, j:j + TA // 2]
                                col = WCOLS + p * (TAPS + 1) + j
                                nc.vector.scalar_tensor_tensor(a, y, w[:, s, col:col + 1], a, ALU.mult, ALU.add)\
                                  .then_inc(tap[p].sem, 1)
                    dve.wait_ge(tap[2].sem, tap[2].at(t, 3 * (s + 1) * NTA))
                    dve.sem_inc(c_used[s].sem, 1)

        @block.scalar
        def _(act):
            act.wait_ge(pads, 4)
            act.wait_ge(var_done, 1)
            nc.scalar.activation(std[:, 0:TT], stat[:, 2 * TT:3 * TT], ACT.Sqrt, bias=eps[:, 0:1]).then_inc(std_done, 1)
            for g in range(4):
                act.wait_ge(xT_ps, g + 1)
                nc.scalar.activation(xT[:, 0, HALO + 512 * g:HALO + 512 * (g + 1)],
                                     psY[g // 2][:, 512 * (g % 2):512 * (g % 2 + 1)], ACT.Copy).then_inc(xT_a, 1)
            act.wait_ge(const_ld, 32)
            for g in range(NTA):
                act.wait_ge(beta_ps, g + 1)
                nc.scalar.activation(beta[:, 512 * g:512 * (g + 1)], psY[g // 2][0:H, 512 * (g % 2):512 * (g % 2 + 1)],
                                     ACT.Sigmoid, bias=bb[:, 0:1]).then_inc(beta_sb, 1)
            act.wait_ge(beta_sb, NTA)
            nc.scalar.activation(nbeta[:], beta[:], ACT.Copy, scale=-1.0).then_inc(nbeta_sb, 1)
            for c in (*ag_free, *ca_used):
                c.start(act)

            with act.Fori(0, TURNS) as t:
                for s in range(2):
                    act.wait_ge(w_ld[s].sem, w_ld[s].at(t, 1))
                    act.wait_ge(st_qkv[s].sem, st_qkv[s].at(t, 0))
                    for i in range(NTA + 1):
                        if i < NTA:
                            n = s * NTA + i
                            for p in range(3):
                                act.wait_ge(y_full[p].sem, y_full[p].at(t, n + 1))
                                col = WCOLS + p * (TAPS + 1)
                                act.wait_ge(silu[p].sem, silu[p].at(t, n - 1))
                                nc.scalar.activation(
                                    acc[:, p, n % 2, :].rearrange("p (b c) -> p b c", b=2),
                                    psY[p][:, :].rearrange("p (b c) -> p b c", b=2)[:, :, HALO:HALO + TA // 2],
                                    ACT.Identity, scale=w[:, s, col + HALO:col + HALO + 1],
                                    bias=w[:, s, col + TAPS:col + TAPS + 1]).then_inc(acc_set[p].sem, 1)
                        if i > 0:
                            n = s * NTA + i - 1
                            for p in range(3):
                                act.wait_ge(tap[p].sem, tap[p].at(t, 3 * (n + 1)))
                                nc.scalar.activation(outs[:, s, p, TA * (i - 1):TA * i], acc[:, p, n % 2, :], ACT.Sigmoid)\
                                  .then_inc(sig[p].sem, 1)
                        if i == NTA:
                            continue
                        if i == 0:
                            act.wait_ge(st_ag.sem, st_ag.at(t, 2 * s))
                        for p in range(2):
                            act.wait_ge(ag_full[p].sem, ag_full[p].at(t, s * NTA + i + 1))
                            bias = w[:, s, WCOLS + CCOLS - 1:WCOLS + CCOLS] if p == 0 else 0.0
                            nc.scalar.activation(outag[:, p, TA * i:TA * (i + 1)], psAG[p][:], ACT.Sigmoid, bias=bias)\
                              .then_inc(ag_free[p].sem, 1)
                    act.wait_ge(ag_free[0].sem, ag_free[0].at(t, (s + 1) * NTA))
                    act.sem_inc(ca_used[s].sem, 1)

        @block.tensor
        def _(pe):
            pe.wait_ge(xn_done, 1)
            for kt in range(KT):
                for g in range(4):
                    n = kt * 4 + g
                    ps = psY[n // 2][:, 512 * (n % 2):512 * (n % 2 + 1)] if n < 6 else psAG[n - 6][:]
                    for m in range(4):
                        last = nc.tensor.transpose(ps[:, 128 * m:128 * (m + 1)],
                                                   xn[:, 4 * g + m, 128 * kt:128 * (kt + 1)], ident[:])
                    last.then_inc(xT_ps, 1)
            pe.wait_ge(pads, 1)
            pe.wait_ge(xT_a, 4)
            pe.wait_ge(xT_v, 4)
            pe.wait_ge(const_ld, 32)
            for g in range(NTA):
                for kt in range(KT):
                    last = nc.tensor.matmul(psY[g // 2][0:H, 512 * (g % 2):512 * (g % 2 + 1)], wb[:, kt, :],
                                            xT[:, kt, HALO + 512 * g:HALO + 512 * (g + 1)],
                                            start=kt == 0, stop=kt == KT - 1)
                last.then_inc(beta_ps, 1)
            pe.wait_ge(beta_sb, NTA)
            w_used[0].start(pe)
            w_used[1].start(pe)
            with pe.Fori(0, TURNS) as t:
                for s in range(2):
                    pe.wait_ge(w_ld[s].sem, w_ld[s].at(t, 1))
                    wp = w[:, s, 0:WCOLS].rearrange("p (j k c) -> p j k c", j=NPROJ, k=KT)
                    for i in range(NTA):
                        n = s * NTA + i
                        for p in range(3):
                            pe.wait_ge(tap[p].sem, tap[p].at(t, 3 * n))
                            for kt in range(KT):
                                for b in range(2):
                                    t0 = i * TA + b * (TA // 2)
                                    last = nc.tensor.matmul(psY[p][:, 512 * b:512 * b + HALO + TA // 2], wp[:, p, kt, :],
                                                            xT[:, kt, t0:t0 + HALO + TA // 2],
                                                            start=kt == 0, stop=kt == KT - 1)
                            last.then_inc(y_full[p].sem, 1)
                        for p in range(2):
                            pe.wait_ge(ag_free[p].sem, ag_free[p].at(t, n))
                            for kt in range(KT):
                                last = nc.tensor.matmul(psAG[p][:], wp[:, A_ + p, kt, :],
                                                        xT[:, kt, HALO + i * TA:HALO + (i + 1) * TA],
                                                        start=kt == 0, stop=kt == KT - 1)
                            last.then_inc(ag_full[p].sem, 1)
                    pe.wait_ge(ag_full[1].sem, ag_full[1].at(t, (s + 1) * NTA))
                    pe.sem_inc(w_used[s].sem, 1)


def leaf_jobs(s, j):
    return {0: [("wo", 0)] if s == 1 else [], 1: [("kk", 1, 0), ("kk", 1, 1)], 2: [("gram", 5)],
            3: [("qk", 0, 0), ("qk", 0, 1), ("qk", 0, 2), ("gram", 6)], 4: [("gram", 7)],
            5: [("ktok", 0), ("ktok", 1)], 6: [("qk", 1, 0), ("qk", 1, 1), ("qk", 1, 2)],
            7: [("decay", 0), ("decay", 1)], 8: [("decay", 2), ("decay", 3)], 9: [("mean", 0), ("mean", 1)],
            10: [("kk", 0, 0), ("kk", 0, 1)], 11: [("var", 0), ("gram", 0)], 12: [("gram", 1), ("gram", 2)],
            13: [("rstd", 0), ("rstd", 1), ("gram", 3)], 14: [("gram", 4)]}.get(j, [])


def turn_jobs():
    out = []
    for s in range(2):
        out += [(s, "contact", i) for i in range(4)]
        for j in range(J):
            out += [(s, *x) for x in leaf_jobs(s, j)]
        out += [(s, "wtok", i) for i in range(2)] + [(s, "update", i) for i in range(4)]
    return out


PROLOGUE = [("first", "kk", 0, 0), ("first", "kk", 0, 1)] + [("first", "gram", i) for i in range(5)]
EPILOGUE = ([("last", "qk", h, i) for h in range(2) for i in range(3)] + [("last", "mean", 0), ("last", "mean", 1),
            ("last", "var", 0), ("last", "rstd", 0), ("last", "rstd", 1), ("last", "wo", 0)])
RING = 5
PAIRS = 6
NCS = 17
DEC = 9


def merge_of(j):
    p = 0
    while (j >> p) & 1:
        p += 1
    return p, R << p, R * (j + 1)


def scale_order():
    out = []
    for b in range(J):
        for p in range(4):
            if b % (2 << p) == 0:
                out.append(b + (1 << p) - 1)
    return out


def gram_places():
    out, n = {}, 0
    for half in range(2):
        js = [j for j in range(8 * half, 8 * half + 8) if j < J - 1]
        for p in range(4):
            tiles = [(j, i) for j in js if merge_of(j)[0] == p for i in range(1 if p == 0 else 1 << (p - 1))]
            width = 128 if p == 0 else 256
            for k, x in enumerate(tiles):
                out[x] = (n + k * width // 512, k * width % 512)
            n += -(-len(tiles) * width // 512)
    return out


def recurrence(nc, ident, scr, nbeta_d, wo_d, lng_d, lnb_d, att_d):
    ctx = ExitStack()
    with ctx:
        sb = lambda name, shape: ctx.enter_context(nc.sbuf_tensor("B_" + name, shape, FP32))
        sem = lambda name: ctx.enter_context(nc.semaphore("B_" + name))
        wo = sb("wo", [128, H, HID])
        lng, lnb, eps = sb("lng", [128, 1]), sb("lnb", [128, 1]), sb("eps", [128, 1])
        ones, avg = sb("ones", [128, 128]), sb("avg", [128, 128])
        masks = sb("masks", [128, 4, 128])
        KQ = sb("KQ", [128, 2, 2, H, C])
        NV, A, G, NB = [sb(x, [128, 2, H, C]) for x in ("NV", "A", "G", "NB")]
        A2 = sb("A2", [128, H, C])
        HC2 = C // 2
        HJ2 = H * J // 2
        KB = sb("KB", [128, H, HC2])
        X = sb("X", [128, PAIRS, HJ2])
        Y = sb("Y", [128, 4 + PAIRS, HJ2])
        RR = sb("RR", [128, 2, H, J])
        F, B = sb("F", [128, 2, H, C]), sb("B", [128, H, C])
        Gs = [sb(f"G{i}", [128, H, J >> i]) for i in range(5)]
        NC = sb("NC", [128, 2, H, J // 2, R * (R + 1)])
        TMP = sb("TMP", [128, H, J // 2, 6])
        ST = sb("ST", [128, H, 128])
        P, Q = sb("P", [128, H, C]), sb("Q", [128, 2, H, C])
        W = sb("W", [128, 2, H, C])
        WT = sb("WT", [128, J, H, R])
        WE = sb("WE", [128, H, C])
        WC = WE[:].rearrange("p h c -> p (h c)")
        KL = sb("KL", [128, J // 2, H, R])
        KC = sb("KC", [128, 3, 256])
        BD = sb("BD", [128, 8, 512])
        KTOK, WTOK = sb("KTOK", [128, 8, 128]), sb("WTOK", [128, 8, 128])
        WL = sb("WL", [128, 512])
        AW = sb("AW", [128, 3, HJ2])
        O, SQ = sb("O", [128, H, C]), sb("SQ", [128, H, C])
        sdev, rdev = sb("sdev", [128, 8]), sb("rdev", [128, 8])
        OG = sb("OG", [128, H, 2 * C])
        att = sb("att", [128, HID])
        ring = [ctx.enter_context(nc.psum_tensor(f"B_ring{i}", [128, 512], FP32)) for i in range(RING)]
        psT = ctx.enter_context(nc.psum_tensor("B_psT", [128, 512], FP32))
        psM = ctx.enter_context(nc.psum_tensor("B_psM", [128, 1024], FP32))

        TURNS = NCH // 2
        JM = J - 1
        grams = gram_places()
        scales = scale_order()
        place = {}
        counts = []
        for part in (PROLOGUE, turn_jobs(), EPILOGUE):
            seen = [0] * RING
            for n, job in enumerate(part):
                place[job] = (n % RING, seen[n % RING])
                seen[n % RING] += 1
            counts.append(seen)
        base, per = counts[0], counts[1]
        full = [Count(sem(f"bank{b}_full"), per[b], 1, 0) for b in range(RING)]
        cl = Count(sem("const_ld"), 3, 16)
        const = Count(sem("const"), 32)
        cst = Count(sem("state_zero"), 1)
        ld = {x: [Count(sem(f"ld_{x}{s}"), 1, 16) for s in range(2)] for x in ("K", "Q", "NV", "A", "G", "NB")}
        kb, xm = Count(sem("kb"), 1), Count(sem("x_made"), 3)
        dec, dcp = Count(sem("decays"), DEC), Count(sem("decay_copies"), 2)
        g4 = Count(sem("g4"), 1)
        nl, nlc = Count(sem("nl"), 2), Count(sem("nl_copy"), 1)
        ncs = Count(sem("leaf_solutions"), NCS)
        bd = Count(sem("grams_masked"), 8)
        ktok, wtok = Count(sem("ktok"), 2, 1, 1), Count(sem("wtok"), 2)
        cont = Count(sem("contact_copied"), 8)
        ap = Count(sem("leaf_terms"), J)
        ws = Count(sem("w_solved"), J, 1, 1)
        wt = Count(sem("w_decayed"), J)
        psc = Count(sem("pq_scaled"), 2 * JM)
        wsc = Count(sem("w_scaled"), JM, 1, 1)
        tps = Count(sem("left_ps"), JM)
        wl = Count(sem("left_copied"), JM, 1, 1)
        kc = Count(sem("k_compact"), 5)
        wc = Count(sem("left_compact"), 3)
        wec = Count(sem("w_end"), 1)
        mps = Count(sem("merge_ps"), JM, 1, 1)
        mg = Count(sem("merged"), 2 * JM, 1, 1)
        stg, stu = Count(sem("state_decayed"), 4), Count(sem("state_updated"), 4, 1, 1)
        a2 = Count(sem("a2_copied"), 1, 1, 0)
        ym = Count(sem("y_made"), 8, 1, 1)
        awm = Count(sem("aw_made"), 4)
        yv = Count(sem("y_terms"), 8)
        om = Count(sem("o_made"), 12)
        oc, sqd = Count(sem("o_centered"), 2), Count(sem("o_squared"), 1)
        sd, rd = Count(sem("sdev"), 1), Count(sem("rdev"), 1)
        on, aff = Count(sem("o_normed"), 2), Count(sem("o_affine"), 1)
        og = Count(sem("o_gated"), 1, 1, 1)
        am, ast = Count(sem("att_made"), 1), Count(sem("att_st"), 1, 16, 1)

        def wait(eng, c, index, k):
            eng.wait_ge(c.sem, c.at(index, k))

        def loaded(eng, what, t, c):
            wait(eng, ld[what][c % 2], t + c // 2, 1)

        def taken(t, label, job):
            kind, n = job[0], job[-1]
            if label == "first":
                return (bd, 0, n + 1) if kind == "gram" else ((nl, 0, 2) if n else (nlc, 0, 1))
            g = NCH if label == "last" else t * 2 + label
            if kind == "kk":
                i = g * 2 + (1 if job[1] else 2)
                return (nl, i, 2) if n else (nlc, i, 1)
            if kind == "gram":
                return bd, g + (n < 5), n + 1
            if kind == "qk":
                return yv, g, 4 * job[1] + (1, 3, 4)[n]
            if kind == "wo":
                return am, t, 1
            return {"contact": (cont, g, n + 5), "ktok": (ktok, g, n + 1), "decay": (stg, g, n + 1), "mean": (oc, g, n + 1),
                    "var": (sd, g, 1), "rstd": (on, g, n + 1), "wtok": (wtok, g, n + 1), "update": (stu, g, n + 1)}[kind]

        parts = {"first": PROLOGUE, "last": EPILOGUE}

        def open_bank(pe, t, label, *job):
            part = parts.get(label, turn_jobs())
            n = part.index((label, *job))
            if n >= RING:
                before, tb = part[n - RING], t
            elif label == "first":
                before = None
            elif label == "last" or not (isinstance(t, int) and t == 0):
                before, tb = [x for m, x in enumerate(turn_jobs()) if m % RING == n][-1], t - 1
            else:
                before, tb = [x for m, x in enumerate(PROLOGUE) if m % RING == n][-1], 0
            if before:
                c, i, k = taken(tb, before[0], before[1:])
                wait(pe, c, i, k)
            b = n % RING
            return ring[b], full[b].sem

        def take_bank(eng, t, label, *job):
            b, k = place[(label, *job)]
            v = k + 1 if label == "first" else (TURNS if label == "last" else t) * per[b] + base[b] + k + 1
            eng.wait_ge(full[b].sem, v)
            return ring[b]

        def leafwise(ap, h):
            return ap[:, :, HC2 * h:HC2 * (h + 1)].rearrange("p h (j r) -> p r h j", r=R)

        def rows(ap):
            return ap.rearrange("p n (h j) -> p n h j", h=H)

        block = ctx.enter_context(nc.Block())

        @block.sync
        def _(sp):
            sp.dma_start(wo[:], wo_d).then_inc(cl.sem, 16)
            sp.dma_start(lng[:], lng_d.rearrange("(p o) -> p o", o=1)).then_inc(cl.sem, 16)
            sp.dma_start(lnb[:], lnb_d.rearrange("(p o) -> p o", o=1)).then_inc(cl.sem, 16)
            ast.start(sp)

            def load(what, s, at):
                dst = {"K": KQ[:, s, 0], "Q": KQ[:, s, 1], "NV": NV[:, s], "A": A[:, s], "G": G[:, s], "NB": NB[:, s]}[what]
                n = {"K": K_, "Q": Q_, "NV": V_, "A": A_, "G": G_}
                src = nbeta_d[:, bass.ds(at, C)].partition_broadcast(128) if what == "NB" else scr[n[what]][:, :, bass.ds(at, C)]
                sp.dma_start(dst, src).then_inc(ld[what][s].sem, 16)

            sp.wait_ge(const.sem, 32)
            for what in ("K", "NB", "NV", "A", "Q", "G"):
                load(what, 0, 0)

            def chunk(t, s, at):
                n = (s + 1) % 2
                g = t * 2 + s
                wait(sp, ncs, t * 4 + 2 * s, 0) if not (isinstance(t, int) and t == 0 and s == 0) else None
                load("NV", n, at)
                load("NB", n, at)
                wait(sp, a2, g, 1)
                load("A", n, at)
                wait(sp, ym, g, 8)
                load("K", n, at)
                load("Q", n, at)
                wait(sp, og, g, 1)
                load("G", n, at)
                if s == 1:
                    wait(sp, am, t, 1)
                    sp.dma_start(att_d[bass.ds(t * (2 * C), 2 * C), :], att[:]).then_inc(ast.sem, 16)

            chunk(0, 0, C)
            chunk(0, 1, 2 * C)
            with sp.Fori(1, TURNS - 1) as t:
                chunk(t, 0, t * (2 * C) + C)
                chunk(t, 1, t * (2 * C) + 2 * C)
            chunk(TURNS - 1, 0, T - C)
            chunk(TURNS - 1, 1, 0)
            wait(sp, am, TURNS, 1)
            sp.dma_start(att_d[TURNS * 2 * C:(TURNS + 1) * 2 * C, :], att[:]).then_inc(ast.sem, 16)
            wait(sp, ast, TURNS, 1)
            for what in ld:
                loaded(sp, what, TURNS, 0)

        @block.gpsimd
        def _(pool):
            tt = nc.gpsimd.tensor_tensor
            nconst = 0
            for ap_, v in ((OG[:], 0.0), (WT[:], 0.0), (ones[:], 1.0), (avg[:], 1.0 / D), (eps[:], EPS), (KQ[:, 1], 0.0), (G[:, 1], 0.0), (A[:, 1], 0.0),
                          (ST[:], 0.0), (W[:, 1], 0.0), (Q[:, 1], 0.0), (RR[:, 1], 0.0), (F[:, 1], 1.0), (F[:, 0], 1.0),
                          (B[:], 1.0), (NC[:], 0.0), (masks[:], 1.0)):
                nc.gpsimd.memset(ap_, v).then_inc(const.sem, 1)
                nconst += 1
            for p in range(4):
                n = 64 if p == 0 else 128
                w_ = R << p
                rw, nr = (R, 2) if p == 1 else (w_, 1)
                for r0 in range(0, n, n // nr):
                    m = masks[r0:r0 + n // nr, p, 0:n].rearrange("p (h t) -> p h t", t=w_)
                    for base_, step, sign in ((0, -rw, 1), (rw - 1, rw, -1)):
                        pool.wait_ge(const.sem, nconst)
                        nc.gpsimd.affine_select(out=m, in_=m, compare_op=ALU.is_ge, fill=0.0, base=base_,
                                                pattern=[[step, n // w_], [0, w_]], channel_multiplier=sign)\
                          .then_inc(const.sem, 1)
                        nconst += 1
            while nconst < 32:
                pool.wait_ge(const.sem, nconst)
                nc.gpsimd.memset(TMP[:, 0:1, 0:1], 0.0).then_inc(const.sem, 1)
                nconst += 1
            for c in (wsc, ym, og):
                c.start(pool)

            def half(t, c4):
                return t * 4 + c4

            def products_kk(t, c4):
                s, h, g = c4 // 2 % 2, c4 % 2, t * 2 + c4 // 2
                loaded(pool, "K", t, c4 // 2)
                loaded(pool, "NB", t, c4 // 2)
                kx = KQ[:, s, 0][:, :, HC2 * h:HC2 * (h + 1)]
                tt(KB[:], kx, NB[:, s, :, HC2 * h:HC2 * (h + 1)], ALU.mult).then_inc(kb.sem, 1)
                wait(pool, kb, half(t, c4), 1)
                if not (isinstance(t, int) and t == 0 and c4 == 0):
                    wait(pool, ncs, half(t, c4), 0)
                kr, br, xr = leafwise(KQ[:, s, 0], h), KB[:].rearrange("p h (j r) -> p r h j", r=R), rows(X[:])
                tt(xr[:, 0:3], br[:, 1:4], kr[:, 0:3], ALU.mult).then_inc(xm.sem, 1)
                tt(xr[:, 3], br[:, 3], kr[:, 0], ALU.mult).then_inc(xm.sem, 1)
                tt(xr[:, 4:6], br[:, 2:4], kr[:, 0:2], ALU.mult).then_inc(xm.sem, 1)

            def decays(t, c4):
                s, h, g = c4 // 2 % 2, c4 % 2, t * 2 + c4 // 2
                i = half(t, c4)
                loaded(pool, "A", t, c4 // 2)
                wait(pool, dcp, i, 2)
                if not (isinstance(t, int) and t == 0 and c4 < 2):
                    wait(pool, wt, t * 2 + c4 // 2 - 1, 8 * h + 8)
                ar, fr, br = leafwise(A[:, s], h), leafwise(F[:, s], h), leafwise(B[:], h)
                J2 = J // 2
                rr = RR[:, s, :, J2 * h:J2 * (h + 1)]
                g0 = Gs[0][:, :, J2 * h:J2 * (h + 1)]
                tt(rr, ar[:, 1], ar[:, 2], ALU.mult).then_inc(dec.sem, 1)
                tt(fr[:, 2], ar[:, 0], ar[:, 1], ALU.mult).then_inc(dec.sem, 1)
                tt(br[:, 1], ar[:, 2], ar[:, 3], ALU.mult).then_inc(dec.sem, 1)
                wait(pool, dec, i, 1)
                tt(br[:, 0], rr, ar[:, 3], ALU.mult).then_inc(dec.sem, 1)
                wait(pool, dec, i, 2)
                tt(fr[:, 3], fr[:, 2], ar[:, 2], ALU.mult).then_inc(dec.sem, 1)
                wait(pool, dec, i, 5)
                tt(g0, fr[:, 3], ar[:, 3], ALU.mult).then_inc(dec.sem, 1)
                for p in (1, 2, 3):
                    wait(pool, dec, i, 5 + p)
                    n = J >> p
                    lo = Gs[p - 1][:, :, n * h:n * (h + 1)].rearrange("p h (j two) -> p two h j", two=2)
                    tt(Gs[p][:, :, n // 2 * h:n // 2 * (h + 1)], lo[:, 0], lo[:, 1], ALU.mult).then_inc(dec.sem, 1)
                if h == 1:
                    wait(pool, dec, i, DEC)
                    if not (isinstance(t, int) and t == 0 and c4 == 1):
                        wait(pool, stg, t * 2 + c4 // 2, 0)
                    tt(Gs[4][:], Gs[3][:, :, 0:1], Gs[3][:, :, 1:2], ALU.mult).then_inc(g4.sem, 1)

            def products_qk(g, s, h):
                kr, qr, yr = leafwise(KQ[:, s, 0], h), leafwise(KQ[:, s, 1], h), rows(Y[:])
                if h == 0:
                    wait(pool, om, g, 0) if not (isinstance(g, int) and g == 0) else None
                else:
                    wait(pool, om, g, 6)
                tt(yr[:, 0:4], qr[:, 0:4], kr[:, 0:4], ALU.mult).then_inc(ym.sem, 1)
                tt(yr[:, 4:7], qr[:, 1:4], kr[:, 0:3], ALU.mult).then_inc(ym.sem, 1)
                tt(yr[:, 7], qr[:, 3], kr[:, 0], ALU.mult).then_inc(ym.sem, 1)
                tt(yr[:, 8:10], qr[:, 2:4], kr[:, 0:2], ALU.mult).then_inc(ym.sem, 1)

            def products_aw(g, s, h):
                wait(pool, a2, g, 1)
                wait(pool, ws, g, 0)
                J2 = J // 2
                wr, ar, awr = leafwise(W[:, s], h), leafwise(A2[:], h), rows(AW[:])
                wait(pool, yv, g, 4 * h) if not (isinstance(g, int) and g == 0 and h == 0) else None
                tt(awr[:, 0], RR[:, s, :, J2 * h:J2 * (h + 1)], wr[:, 0], ALU.mult).then_inc(awm.sem, 1)
                tt(awr[:, 1:3], ar[:, 1:3], wr[:, 0:2], ALU.mult).then_inc(awm.sem, 1)
                if h == 0:
                    wait(pool, og, g, 0)
                x = slice(HC2 * h, HC2 * (h + 1))
                wait(pool, mg, g, 0)
                tt(O[:, :, x], Q[:, s, :, x], F[:, s, :, x], ALU.mult).then_inc(om.sem, 1)

            def outputs(g, s, h):
                orr, yr, x = leafwise(O[:], h), rows(Y[:]), slice(HC2 * h, HC2 * (h + 1))
                i = 6 * h
                wait(pool, yv, g, 4 * h + 4)
                wait(pool, om, g, i + 1)
                tt(orr[:, 1:4], orr[:, 1:4], yr[:, 4:7], ALU.add).then_inc(om.sem, 1)
                wait(pool, om, g, i + 2)
                tt(orr[:, 3], orr[:, 3], yr[:, 7], ALU.add).then_inc(om.sem, 1)
                wait(pool, om, g, i + 3)
                tt(orr[:, 2:4], orr[:, 2:4], yr[:, 8:10], ALU.add).then_inc(om.sem, 1)
                wait(pool, om, g, i + 4)
                tt(O[:, :, x], O[:, :, x], A2[:, :, x], ALU.mult).then_inc(om.sem, 1)
                wait(pool, om, g, i + 5)
                tt(orr[:, 0:4], orr[:, 0:4], yr[:, 0:4], ALU.add).then_inc(om.sem, 1)

            def gate(t, g, s):
                wait(pool, aff, g, 1)
                if not (isinstance(g, int) and g == 0):
                    loaded(pool, "G", t, -s)
                if s == 0:
                    wait(pool, am, t, 1)
                tt(OG[:, :, C * s:C * (s + 1)], SQ[:], G[:, s], ALU.mult).then_inc(og.sem, 1)

            def scale_right(t, s, b):
                g = t * 2 + s
                for j in [b + (1 << p) - 1 for p in range(4) if b % (2 << p) == 0]:
                    p, n, r0 = merge_of(j)
                    if b == 0:
                        wait(pool, dec, 2 * g, DEC)
                        wait(pool, cont, g, 8)
                    else:
                        wait(pool, mg, g, 2 * b)
                    gl = Gs[p][:, :, b >> p:(b >> p) + 1].to_broadcast([128, H, n])
                    for dst in (P[:, :, r0:r0 + n], Q[:, s, :, r0:r0 + n]):
                        tt(dst, dst, gl, ALU.mult).then_inc(psc.sem, 1)

            def scale_left(t, s, j):
                g = t * 2 + s
                p, n, r0 = merge_of(j)
                if j >= 7:
                    wait(pool, dec, 2 * g + 1, DEC)
                wait(pool, tps, g, j + 1)
                wait(pool, wsc, g, j)
                gr = Gs[p][:, :, (r0 // R) >> p].unsqueeze(1).unsqueeze(3).to_broadcast([128, n // R, H, R])
                dst = WT[:, (r0 - n) // R:r0 // R]
                tt(dst, dst, gr, ALU.mult).then_inc(wsc.sem, 1)

            def chunk(t, s):
                g, o = t * 2 + s, (s + 1) % 2
                for j in range(J):
                    if j == 0:
                        scale_right(t, s, 0)
                    if j == 0:
                        products_kk(t, 2 * s + 1)
                    elif j == 1:
                        decays(t, 2 * s + 1)
                    elif j == 2:
                        products_qk(g, o, 0)
                    elif j == 3:
                        products_aw(g, o, 0)
                    elif j == 5:
                        outputs(g, o, 0)
                        products_qk(g, o, 1)
                        products_aw(g, o, 1)
                    elif j == 8:
                        outputs(g, o, 1)
                    elif j == 9:
                        products_kk(t, 2 * s + 2)
                    elif j == 10:
                        decays(t, 2 * s + 2)
                    elif j == 15:
                        gate(t, g, o)
                    if j < JM:
                        scale_left(t, s, j)
                        if j + 1 < J:
                            scale_right(t, s, j + 1)

            def last_outputs(g):
                products_qk(g, 1, 0)
                products_aw(g, 1, 0)
                outputs(g, 1, 0)
                products_qk(g, 1, 1)
                products_aw(g, 1, 1)
                outputs(g, 1, 1)
                gate(TURNS, g, 1)

            products_kk(0, 0)
            decays(0, 0)
            chunk(0, 0)
            chunk(0, 1)
            with pool.Fori(1, TURNS) as t:
                chunk(t, 0)
                chunk(t, 1)
            last_outputs(NCH)

        @block.vector
        def _(dve):
            tt = nc.vector.tensor_tensor
            for c in (ws, mg, stu):
                c.start(dve)
            dve.wait_ge(const.sem, 32)

            def row_pairs(t, c4, label):
                s, h, i = c4 // 2 % 2, c4 % 2, t * 4 + c4
                J2 = J // 2
                xr, ar = rows(X[:]), leafwise(A[:, s], h)
                wait(dve, dec, i, 1)
                loaded(dve, "A", t, c4 // 2)
                ps = take_bank(dve, t, label, "kk", h, 1)
                pr = ps[:, 0:3 * HJ2].rearrange("p (n h j) -> p n h j", n=3, h=H)
                tt(xr[:, 3], pr[:, 0], RR[:, s, :, J2 * h:J2 * (h + 1)], ALU.mult).then_inc(nl.sem, 1)
                tt(xr[:, 4:6], pr[:, 1:3], ar[:, 1:3], ALU.mult).then_inc(nl.sem, 1)

            def leaf_solution(t, c4, part):
                s, h, i = c4 // 2 % 2, c4 % 2, t * 4 + c4
                g = t * 2 + c4 // 2
                xr, n = rows(X[:]), NC[:, h]

                def row(t_, a, b):
                    return n[:, :, :, 5 * t_ + a:5 * t_ + b]

                def coef(k, cols):
                    return xr[:, k].unsqueeze(3).to_broadcast([128, H, J // 2, cols])

                def step(k, need, out, in0, in1, op):
                    if need:
                        wait(dve, ncs, i, need)
                    tt(out, in0, in1, op).then_inc(ncs.sem, 1)

                x = slice(HC2 * h, HC2 * (h + 1))
                by_leaf = lambda ap: ap.rearrange("p h (j r) -> p h j r", r=R)
                if part == 0:
                    wait(dve, dec, i, DEC)
                    loaded(dve, "NB", t, c4 // 2)
                    loaded(dve, "NV", t, c4 // 2)
                    step(1, 0, n[:, :, :, 1::6], by_leaf(NB[:, s, :, x]), by_leaf(F[:, s, :, x]), ALU.mult)
                    step(2, 0, n[:, :, :, 0::5], by_leaf(NB[:, s, :, x]), by_leaf(NV[:, s, :, x]), ALU.mult)
                elif part == 1:
                    wait(dve, nlc, i, 1)
                    wait(dve, nl, i, 2)
                    step(3, 1, row(1, 1, 2), coef(0, 1), row(0, 1, 2), ALU.mult)
                    step(4, 2, TMP[:, :, :, 0:1], coef(0, 1), row(0, 0, 1), ALU.mult)
                    step(5, 4, row(1, 0, 1), row(1, 0, 1), TMP[:, :, :, 0:1], ALU.add)
                    step(6, 0, TMP[:, :, :, 1:3], coef(4, 2), row(0, 0, 2), ALU.mult)
                    step(7, 0, row(2, 1, 3), coef(1, 2), row(1, 1, 3), ALU.mult)
                elif part == 2:
                    step(8, 7, TMP[:, :, :, 0:1], coef(1, 1), row(1, 0, 1), ALU.mult)
                    step(9, 8, row(2, 0, 1), row(2, 0, 1), TMP[:, :, :, 0:1], ALU.add)
                    step(10, 9, row(2, 0, 2), row(2, 0, 2), TMP[:, :, :, 1:3], ALU.add)
                    step(11, 10, row(3, 1, 4), coef(2, 3), row(2, 1, 4), ALU.mult)
                    step(12, 0, TMP[:, :, :, 0:1], coef(2, 1), row(2, 0, 1), ALU.mult)
                else:
                    step(13, 12, row(3, 0, 1), row(3, 0, 1), TMP[:, :, :, 0:1], ALU.add)
                    step(14, 0, TMP[:, :, :, 3:6], coef(5, 3), row(1, 0, 3), ALU.mult)
                    step(15, 14, row(3, 0, 3), row(3, 0, 3), TMP[:, :, :, 3:6], ALU.add)
                    step(16, 0, TMP[:, :, :, 1:3], coef(3, 2), row(0, 0, 2), ALU.mult)
                    step(17, 16, row(3, 0, 2), row(3, 0, 2), TMP[:, :, :, 1:3], ALU.add)

            def mask_gram(t, label, i):
                ps = take_bank(dve, t, label, "gram", i)
                p = min(q for (j, k), (b, c) in grams.items() if b == i for q in [merge_of(j)[0]])
                if p == 0:
                    n, m = 8, masks[0:64, 0, 0:64]
                    rs = 64
                else:
                    n, m, rs = 4, masks[:, p, :], 128
                v = lambda ap: ap.rearrange("p (n c) -> p n c", n=n)
                tt(v(BD[0:rs, i, :]), v(ps[0:rs, :]), m.unsqueeze(1).to_broadcast([rs, n, 512 // n]), ALU.mult)\
                    .then_inc(bd.sem, 1)

            def terms_qk(t, g, label, s, h):
                wr, yr, awr = leafwise(W[:, s], h), rows(Y[:]), rows(AW[:])
                v = lambda ps, n: ps[:, 0:n * HJ2].rearrange("p (n h j) -> p n h j", n=n, h=H)
                wait(dve, ws, g, 0)
                wait(dve, awm, g, 2 * h + 2)
                ps = take_bank(dve, t, label, "qk", h, 0)
                tt(yr[:, 0:4], v(ps, 4), wr[:, 0:4], ALU.mult).then_inc(yv.sem, 1)
                ps = take_bank(dve, t, label, "qk", h, 1)
                tt(yr[:, 4:7], v(ps, 4)[:, 0:3], wr[:, 0:3], ALU.mult).then_inc(yv.sem, 1)
                tt(yr[:, 7], v(ps, 4)[:, 3], awr[:, 0], ALU.mult).then_inc(yv.sem, 1)
                ps = take_bank(dve, t, label, "qk", h, 2)
                tt(yr[:, 8:10], v(ps, 2), awr[:, 1:3], ALU.mult).then_inc(yv.sem, 1)

            def center(t, g, label):
                for i in range(2):
                    ps = take_bank(dve, t, label, "mean", i)
                    o = O[:, 8 * i:8 * (i + 1), :]
                    tt(o, o, ps[:].rearrange("p (h c) -> p h c", h=8), ALU.subtract).then_inc(oc.sem, 1)

            def invert(g):
                wait(dve, sd, g, 1)
                nc.vector.reciprocal(rdev[:], sdev[:]).then_inc(rd.sem, 1)

            def norm(t, g, label):
                for i in range(2):
                    ps = take_bank(dve, t, label, "rstd", i)
                    o = O[:, 8 * i:8 * (i + 1), :]
                    tt(o, o, ps[:].rearrange("p (h c) -> p h c", h=8), ALU.mult).then_inc(on.sem, 1)

            def decay_state(t, g, s, i):
                wait(dve, cont, g, 8)
                ps = take_bank(dve, t, s, "decay", i)
                x = ST[:, 4 * i:4 * i + 4, :]
                tt(x, x, ps[:].rearrange("p (h v) -> p h v", h=4), ALU.mult).then_inc(stg.sem, 1)

            def chunk(t, s):
                g, o = t * 2 + s, (s + 1) % 2
                first = isinstance(t, int) and t == 0 and s == 0
                nxt = 2 * s + 2
                if not first:
                    wait(dve, om, g, 0)
                for j in range(J):
                    jj, h = j % 8, j // 8
                    if j == 0 or j == 8:
                        wait(dve, ncs, 2 * g + h, NCS)
                    lf = slice(R * j, R * (j + 1))
                    eq = NC[:, h, :, jj, :].rearrange("p h (t c) -> p h t c", c=R + 1)
                    if j == 0:
                        wait(dve, cont, g, 4)
                    else:
                        wait(dve, mg, g, 2 * j - 1)
                    tt(eq[:, :, :, 1:5], eq[:, :, :, 1:5], P[:, :, lf].unsqueeze(2).to_broadcast([128, H, R, R]), ALU.mult)\
                        .then_inc(ap.sem, 1)
                    wait(dve, ap, g, j + 1)
                    nc.vector.tensor_reduce(W[:, s, :, lf], eq, AXIS.X, ALU.add).then_inc(ws.sem, 1)
                    wait(dve, ws, g, j + 1)
                    tt(WT[:, j], W[:, s, :, lf], B[:, :, lf], ALU.mult).then_inc(wt.sem, 1)

                    if j == 2:
                        row_pairs(t, 2 * s + 1, s)
                        leaf_solution(t, 2 * s + 1, 0)
                    elif j == 3:
                        mask_gram(t, s, 5)
                        leaf_solution(t, 2 * s + 1, 1)
                    elif j == 4:
                        terms_qk(t, g, s, o, 0)
                        mask_gram(t, s, 6)
                    elif j == 5:
                        leaf_solution(t, 2 * s + 1, 2)
                        mask_gram(t, s, 7)
                    elif j == 6:
                        leaf_solution(t, 2 * s + 1, 3)
                    elif j == 7:
                        terms_qk(t, g, s, o, 1)
                    elif j == 8:
                        decay_state(t, g, s, 0)
                        decay_state(t, g, s, 1)
                    elif j == 9:
                        decay_state(t, g, s, 2)
                        decay_state(t, g, s, 3)
                    elif j == 10:
                        center(t, g, s)
                    elif j == 11:
                        row_pairs(t, nxt, s)
                        leaf_solution(t, nxt, 0)
                    elif j == 12:
                        mask_gram(t, s, 0)
                        leaf_solution(t, nxt, 1)
                    elif j == 13:
                        invert(g)
                        mask_gram(t, s, 1)
                        mask_gram(t, s, 2)
                        leaf_solution(t, nxt, 2)
                    elif j == 14:
                        norm(t, g, s)
                        mask_gram(t, s, 3)
                    elif j == 15:
                        leaf_solution(t, nxt, 3)
                        mask_gram(t, s, 4)

                    if j < JM:
                        p, n, r0 = merge_of(j)
                        tiles, hp = (1, H) if p == 0 else (1 << (p - 1), 128 // n)
                        m = psM[:, 0:tiles * 2 * hp * n].rearrange("p (i q h t) -> p i q h t", i=tiles, q=2, h=hp)
                        v = lambda ap: ap.rearrange("p (i h) t -> p i h t", i=tiles)
                        wait(dve, mps, g, j + 1)
                        k = 2 * scales.index(j)
                        wait(dve, psc, g, k + 1)
                        x = v(P[:, :, r0:r0 + n])
                        tt(x, x, m[:, :, 0], ALU.add).then_inc(mg.sem, 1)
                        wait(dve, psc, g, k + 2)
                        x = v(Q[:, s, :, r0:r0 + n])
                        tt(x, x, m[:, :, 1], ALU.add).then_inc(mg.sem, 1)
                wait(dve, stg, g, 4)
                for i in range(4):
                    ps = take_bank(dve, t, s, "update", i)
                    x = ST[:, i % 2 + 8 * (i // 2):8 * (i // 2) + 8:2, :]
                    tt(x, x, ps[:].rearrange("p (h v) -> p h v", h=4), ALU.add).then_inc(stu.sem, 1)

            row_pairs(0, 0, "first")
            for part in range(4):
                leaf_solution(0, 0, part)
            for i in range(5):
                mask_gram(0, "first", i)
            chunk(0, 0)
            chunk(0, 1)
            with dve.Fori(1, TURNS) as t:
                chunk(t, 0)
                chunk(t, 1)
            dve.wait_ge(om.sem, om.at(NCH, 0))
            for h in range(2):
                terms_qk(TURNS, NCH, "last", 1, h)
            center(TURNS, NCH, "last")
            invert(NCH)
            norm(TURNS, NCH, "last")

        @block.scalar
        def _(act):
            copy = lambda out, in_: nc.scalar.activation(out, in_, ACT.Copy)
            for c in (ktok, wl):
                c.start(act)
            act.wait_ge(const.sem, 32)
            act.wait_ge(cl.sem, cl.at(0, 3))

            def decay_copies(t, c4):
                s, h, g = c4 // 2 % 2, c4 % 2, t * 2 + c4 // 2
                loaded(act, "A", t, c4 // 2)
                if not (isinstance(t, int) and t == 0 and c4 < 2):
                    wait(act, ncs, t * 4 + c4 - 1, 0)
                    wait(act, wt, g - 1, 8 * h + 8)
                    wait(act, om, g - 1, 7)
                ar = leafwise(A[:, s], h)
                copy(leafwise(F[:, s], h)[:, 1], ar[:, 0]).then_inc(dcp.sem, 1)
                copy(leafwise(B[:], h)[:, 2], ar[:, 3]).then_inc(dcp.sem, 1)

            def k_compact(t, c4):
                s, h, g = c4 // 2 % 2, c4 % 2, t * 2 + c4 // 2
                loaded(act, "K", t, c4 // 2)
                if not (isinstance(t, int) and t == 0 and c4 == 0):
                    wait(act, bd, g, 5) if h else wait(act, bd, g, 0)
                kx, c0 = KQ[:, s, 0], HC2 * h
                copy(KL[:], kx[:, :, c0:c0 + HC2].rearrange("p h (j r) -> p j h r", r=R)).then_inc(kc.sem, 1)
                copy(KC[:, 0].rearrange("p (h t) -> p h t", h=H), kx[:, :, c0:c0 + 16]).then_inc(kc.sem, 1)
                if h == 0:
                    copy(KC[:, 1:3].rearrange("p n (h t) -> p (n h) t", t=32), kx[:, :, 0:32]).then_inc(kc.sem, 1)

            def pairs_copy(t, c4, label):
                ps = take_bank(act, t, label, "kk", c4 % 2, 0)
                copy(X[:, 0:3, :].rearrange("p n c -> p (n c)"), ps[:, 0:3 * HJ2]).then_inc(nlc.sem, 1)

            def contact_copy(t, s):
                g = t * 2 + s
                if not (isinstance(t, int) and t == 0 and s == 0):
                    wait(act, mg, g, 0)
                    wait(act, ws, g, 0)
                    wait(act, om, g, 0)
                for q in range(2):
                    for i in range(4):
                        ps = take_bank(act, t, s, "contact", i)
                        dst = (P[:], Q[:, s])[q][:, 4 * i:4 * i + 4, :]
                        copy(dst, ps[:].rearrange("p (h q t) -> p q h t", h=4, q=2)[:, q]).then_inc(cont.sem, 1)

            def squares(t, g):
                wait(act, oc, g, 2)
                wait(act, og, g, 0)
                nc.scalar.activation(SQ[:], O[:], ACT.Square).then_inc(sqd.sem, 1)

            def deviation(t, g, label):
                ps = take_bank(act, t, label, "var", 0)
                if not (isinstance(g, int) and g == 0):
                    wait(act, rd, g, 0)
                nc.scalar.activation(sdev[:], ps[:, 0:8], ACT.Sqrt, bias=eps[:, 0:1]).then_inc(sd.sem, 1)

            def affine(g):
                wait(act, on, g, 2)
                nc.scalar.activation(SQ[:], O[:], ACT.Identity, scale=lng[:, 0:1], bias=lnb[:, 0:1]).then_inc(aff.sem, 1)

            def att_copy(t, label):
                ps = take_bank(act, t, label, "wo", 0)
                if not (isinstance(t, int) and t == 0):
                    wait(act, ast, t, 0)
                copy(att[:], ps[:, 0:HID]).then_inc(am.sem, 1)

            def chunk(t, s):
                g, o = t * 2 + s, (s + 1) % 2
                first = isinstance(t, int) and t == 0 and s == 0
                contact_copy(t, s)
                for j in range(J):
                    if j < JM:
                        p, n, r0 = merge_of(j)
                        if p >= 2:
                            wait(act, wt, g, j + 1)
                            wait(act, wsc, g, j)
                            wait(act, tps, g, j)
                            copy(WC[:, 0:H * n].rearrange("p (h l r) -> p h l r", h=H, r=R),
                                 WT[:, (r0 - n) // R:r0 // R].rearrange("p l h r -> p h l r")).then_inc(wc.sem, 1)
                        wait(act, tps, g, j + 1)
                        wait(act, mps, g, j)
                        w_ = 128 << max(p - 1, 0)
                        copy(WL[:, 0:w_], psT[:, 0:w_]).then_inc(wl.sem, 1)
                    if j == 0:
                        decay_copies(t, 2 * s + 1)
                        k_compact(t, 2 * s + 1)
                        if not first:
                            loaded(act, "A", t, s - 1)
                            wait(act, om, g, 0)
                        copy(A2[:], A[:, o]).then_inc(a2.sem, 1)
                    elif j == 1 and s == 1:
                        att_copy(t, s)
                    elif j == 2:
                        pairs_copy(t, 2 * s + 1, s)
                    elif j == 6:
                        for i in range(2):
                            ps = take_bank(act, t, s, "ktok", i)
                            wait(act, stu, g, 0)
                            copy(KTOK[:, 4 * i:4 * i + 4, :].rearrange("p n c -> p (n c)"), ps[:]).then_inc(ktok.sem, 1)
                    elif j == 9:
                        decay_copies(t, 2 * s + 2)
                        k_compact(t, 2 * s + 2)
                    elif j == 10:
                        squares(t, g)
                    elif j == 11:
                        pairs_copy(t, 2 * s + 2, s)
                    elif j == 12:
                        deviation(t, g, s)
                    elif j == 14:
                        affine(g)
                wait(act, wt, g, J)
                wait(act, wsc, g, JM)
                copy(WE[:].rearrange("p h (l r) -> p h l r", r=R), WT[:].rearrange("p l h r -> p h l r")).then_inc(wec.sem, 1)
                for i in range(2):
                    ps = take_bank(act, t, s, "wtok", i)
                    wait(act, stu, g, 0)
                    copy(WTOK[:, 4 * i:4 * i + 4, :].rearrange("p n c -> p (n c)"), ps[:]).then_inc(wtok.sem, 1)

            decay_copies(0, 0)
            k_compact(0, 0)
            pairs_copy(0, 0, "first")
            chunk(0, 0)
            chunk(0, 1)
            with act.Fori(1, TURNS) as t:
                chunk(t, 0)
                chunk(t, 1)
            loaded(act, "A", TURNS, -1)
            wait(act, om, NCH, 0)
            copy(A2[:], A[:, 1]).then_inc(a2.sem, 1)
            squares(TURNS, NCH)
            deviation(TURNS, NCH, "last")
            affine(NCH)
            att_copy(TURNS, "last")

        @block.tensor
        def _(pe):
            mm = nc.tensor.matmul
            for c in (mps,):
                c.start(pe)
            pe.wait_ge(const.sem, 32)
            pe.wait_ge(cl.sem, cl.at(0, 3))

            def shared_job(t, label, job):
                kind, n = job[0], job[-1]
                g = NCH if label == "last" else (0 if label == "first" else t * 2 + label)
                s = 1 if label == "last" else (0 if label == "first" else label)
                ps, filled = open_bank(pe, t, label, *job)
                if kind == "contact":
                    wait(pe, stu, g, 4 * (0) - 2 if n < 2 else 0)
                    if n == 0:
                        loaded(pe, "K", t, s)
                        loaded(pe, "Q", t, s)
                    for m in range(4):
                        h = 4 * n + m
                        last = mm(ps[:, 128 * m:128 * (m + 1)], ST[:, h, :], KQ[:, s, :, h, :], start=True, stop=True)
                elif kind == "kk":
                    i = 0 if label == "first" else g * 2 + (1 if job[1] else 2)
                    wait(pe, xm, i, 3)
                    last = mm(ps[:, 0:3 * HJ2], ones[:], X[:, 3 * n:3 * n + 3, :].rearrange("p n c -> p (n c)"),
                              start=True, stop=True)
                elif kind == "gram":
                    gs, gi = (s, g) if (n >= 5 or label == "first") else ((s + 1) % 2, g + 1)
                    ci = 0 if label == "first" else label + (n < 5)
                    loaded(pe, "K", t, ci)
                    loaded(pe, "Q", t, ci)
                    wait(pe, kc, gi, 3 if n < 5 else 5)
                    for (j, i), (bank, col) in grams.items():
                        if bank != n:
                            continue
                        p, w_, r0 = merge_of(j)
                        hp = H if p == 0 else 128 // w_
                        hs = slice(i * hp, (i + 1) * hp)
                        rs = hp * w_
                        l0 = (r0 - w_) % HC2 // R
                        if p < 2:
                            left = KL[:, l0:l0 + w_ // R].rearrange("p l h r -> p (l h r)")
                        else:
                            left = KC[:].rearrange("p n c -> p (n c)")[:, (256 if p == 3 else 0) + rs * i:][:, 0:rs]
                        last = mm(ps[0:rs, col:col + 2 * rs], left, KQ[:, gs, :, hs, r0:r0 + w_],
                                  start=True, stop=True)
                elif kind == "ktok":
                    for m in range(4):
                        i = 4 * n + m
                        last = nc.tensor.transpose(ps[:, 128 * m:128 * (m + 1)], KQ[:, s, 0, 2 * i:2 * i + 2, :].rearrange("p h c -> p (h c)"), ident[:])
                elif kind == "decay":
                    wait(pe, g4, g, 1)
                    for m in range(4):
                        last = mm(ps[:, 128 * m:128 * (m + 1)], Gs[4][:, 4 * n + m, :].to_broadcast([128, 128]), ident[:],
                                  start=True, stop=True)
                elif kind == "qk":
                    h = job[1]
                    wait(pe, ym, g, 4 * h + 4)
                    a, b = ((0, 4), (4, 8), (8, 10))[n]
                    last = mm(ps[:, 0:(b - a) * HJ2], ones[:], Y[:, a:b, :].rearrange("p n c -> p (n c)"), start=True, stop=True)
                elif kind == "mean":
                    wait(pe, om, g, 12)
                    last = mm(ps[:], avg[:], O[:, 8 * n:8 * n + 8, :].rearrange("p h c -> p (h c)"), start=True, stop=True)
                elif kind == "var":
                    wait(pe, sqd, g, 1)
                    for i in range(8):
                        last = mm(ps[:, i:i + 1], SQ[:, 2 * i:2 * i + 2, :].rearrange("p h c -> p (h c)"), avg[:, 0:1],
                                  start=True, stop=True)
                elif kind == "rstd":
                    wait(pe, rd, g, 1)
                    for m in range(4):
                        i = 4 * n + m
                        last = mm(ps[:, 128 * m:128 * (m + 1)], rdev[:, i:i + 1].to_broadcast([128, 128]), ident[:],
                                  start=True, stop=True)
                elif kind == "wo":
                    wait(pe, og, g, 1 if label == "last" else 0)
                    for h in range(H):
                        last = mm(ps[:, 0:HID], OG[:, h, :], wo[:, h, :], start=h == 0, stop=h == H - 1)
                elif kind == "wtok":
                    wait(pe, wec, g, 1)
                    for m in range(4):
                        i = 4 * n + m
                        last = nc.tensor.transpose(ps[:, 128 * m:128 * (m + 1)],
                                                   WE[:, 2 * i:2 * i + 2, :].rearrange("p h c -> p (h c)"), ident[:])
                elif kind == "update":
                    wait(pe, wtok, g, n // 2 + 1)
                    wait(pe, ktok, g, 2)
                    r = slice(64 * (n % 2), 64 * (n % 2) + 64)
                    for m in range(4):
                        i = 4 * (n // 2) + m
                        last = mm(ps[:, 128 * m:128 * (m + 1)], KTOK[r, i, :], WTOK[r, i, :], start=True, stop=True)
                last.then_inc(filled, 1)

            def chunk(t, s):
                g = t * 2 + s
                for i in range(4):
                    shared_job(t, s, ("contact", i))
                for j in range(J):
                    if j < JM:
                        p, n, r0 = merge_of(j)
                        tiles, hp = (1, H) if p == 0 else (1 << (p - 1), 128 // n)
                        rs = hp * n
                        wait(pe, wt, g, j + 1)
                        if p == 1:
                            wait(pe, wsc, g, j)
                        elif p >= 2:
                            wait(pe, wc, g, {3: 1, 7: 2, 11: 3}[j])
                        wait(pe, wl, g, j)
                        for i in range(tiles):
                            left = (WT[:, j - p:j - p + 2].rearrange("p l h r -> p (l h r)") if p < 2
                                    else WC[:, 128 * i:128 * (i + 1)])
                            last = nc.tensor.transpose(psT[:, 128 * i:128 * (i + 1)], left, ident[:])
                        last.then_inc(tps.sem, 1)
                        if j == 0:
                            wait(pe, bd, g, 5)
                        elif j == 8:
                            wait(pe, bd, g, 8)
                        wait(pe, wl, g, j + 1)
                        wait(pe, mg, g, 2 * j)
                        for i in range(tiles):
                            bank, col = grams[j, i]
                            last = mm(psM[:, 2 * rs * i:2 * rs * (i + 1)], WL[0:rs, 128 * i:128 * (i + 1)],
                                      BD[0:rs, bank, col:col + 2 * rs], start=True, stop=True)
                        last.then_inc(mps.sem, 1)
                    for job in leaf_jobs(s, j):
                        shared_job(t, s, job)
                for i in range(2):
                    shared_job(t, s, ("wtok", i))
                for i in range(4):
                    shared_job(t, s, ("update", i))

            for job in PROLOGUE:
                shared_job(0, "first", job[1:])
            chunk(0, 0)
            chunk(0, 1)
            with pe.Fori(1, TURNS) as t:
                chunk(t, 0)
                chunk(t, 1)
            for job in EPILOGUE:
                shared_job(TURNS, "last", job[1:])


def feed_forward(nc, ident, x_d, att_d, gate_d, gbias_d, wg_d, wu_d, wd_d, out_d):
    ctx = ExitStack()
    with ctx:
        sb = lambda name, shape: ctx.enter_context(nc.sbuf_tensor("C_" + name, shape, FP32))
        sem = lambda name: ctx.enter_context(nc.semaphore("C_" + name))
        NT = TF // 128
        wg, wu = sb("wg", [128, KT, HROWS]), sb("wu", [128, KT, HROWS])
        wd = sb("wd", [128, MT, HID])
        gate, gbias = sb("gate", [128, KT, E]), sb("gbias", [128, E])
        eps = sb("eps", [128, 1])
        spread = sb("spread", [E, E * HE])
        rank = sb("rank", [128, NT, E])
        x, at = sb("x", [128, 2, NT, HID]), sb("at", [128, 2, NT, HID])
        x1, xc, xn = sb("x1", [128, NT, HID]), sb("xc", [128, NT, HID]), sb("xn", [128, NT, HID])
        stat, std = sb("stat", [128, 3 * NT]), sb("std", [128, 2 * NT])
        xT = sb("xT", [128, KT, TF])
        score = sb("score", [128, NT, E])
        key, pick, tmp, wsel = [sb(n, [128, NT, E]) for n in ("key", "pick", "tmp", "wsel")]
        best, inv = sb("best", [128, NT]), sb("inv", [128, NT])
        wT = sb("wT", [E, TF])
        act_g = sb("act_g", [128, 2, TF])
        hid = sb("hid", [128, MT, TF])
        y = sb("y", [128, NT, HID])
        psG = [ctx.enter_context(nc.psum_tensor(f"C_psG{i}", [128, 512], FP32)) for i in range(2)]
        psU = [ctx.enter_context(nc.psum_tensor(f"C_psU{i}", [128, 512], FP32)) for i in range(2)]
        psW = [ctx.enter_context(nc.psum_tensor(f"C_psW{i}", [128, 512], FP32)) for i in range(2)]
        psX = [ctx.enter_context(nc.psum_tensor(f"C_psX{i}", [128, 512], FP32)) for i in range(2)]
        w_ld, const = sem("w_ld"), sem("const")
        x_ld = [Count(sem(f"x_ld{s}"), 2, 16) for s in range(2)]
        ROUTE = 19
        x1m, ln, var = Count(sem("x1_made"), 1), Count(sem("ln"), 6), Count(sem("var"), 1)
        sd, xnm = Count(sem("std"), 1), Count(sem("xn_made"), 1)
        xtp, xtm = Count(sem("xT_ps"), 2), Count(sem("xT_made"), 2)
        gp, sc = Count(sem("gate_ps"), 1), Count(sem("score"), 1)
        rt = Count(sem("routing"), ROUTE)
        wp, wm = Count(sem("weights_ps"), 1), Count(sem("weights_made"), 1)
        gu, gs = Count(sem("hidden_ps"), MT), Count(sem("silu"), MT)
        wb = Count(sem("spread_ps"), ET)
        hm, hw = Count(sem("hidden"), MT, 1, 1), Count(sem("hidden_weighted"), ET, 1, 1)
        dn, ym = Count(sem("down_ps"), NT), Count(sem("y_made"), NT, 1, 1)
        st = Count(sem("out_st"), 1, 16, 1)
        order = list(range(ET, MT)) + list(range(ET))

        def wait(eng, c, index, k):
            eng.wait_ge(c.sem, c.at(index, k))

        block = ctx.enter_context(nc.Block())

        @block.sync
        def _(sp):
            st.start(sp)

            def load(t, s, at0):
                for dst, src in ((x, x_d), (at, att_d)):
                    sp.dma_start(dst[:, s], src[bass.ds(at0, TF), :].rearrange("(n p) c -> p n c", p=128))\
                      .then_inc(x_ld[s].sem, 16)

            load(0, 0, 0)
            sp.dma_start(gate[:], gate_d.rearrange("(k p) e -> p k e", p=128)).then_inc(w_ld, 16)
            sp.dma_start(gbias[:], gbias_d.partition_broadcast(128)).then_inc(w_ld, 16)
            sp.dma_start(wg[:], wg_d.rearrange("(k p) n -> p k n", p=128)).then_inc(w_ld, 16)
            sp.dma_start(wu[:], wu_d.rearrange("(k p) n -> p k n", p=128)).then_inc(w_ld, 16)
            sp.dma_start(wd[:, 0:MT - 1, :], wd_d[0:128 * (MT - 1), :].rearrange("(m p) c -> p m c", p=128)).then_inc(w_ld, 16)
            sp.dma_start(wd[0:MROWS[-1], MT - 1, :], wd_d[128 * (MT - 1):HROWS, :]).then_inc(w_ld, 16)
            load(0, 1, TF)
            with sp.Fori(0, NTF // 2) as t:
                for s in range(2):
                    i = t * 2 + s
                    wait(sp, ym, i, NT)
                    sp.dma_start(out_d[bass.ds(t * (2 * TF) + s * TF, TF), :].rearrange("(n p) c -> p n c", p=128), y[:])\
                      .then_inc(st.sem, 16)
                    sp.wait_ge(x1m.sem, x1m.at(i, 1))
                    for dst, src in ((x, x_d), (at, att_d)):
                        sp.dma_start(dst[:, s], src[bass.ds(((t + 1) % (NTF // 2)) * (2 * TF) + s * TF, TF), :]
                                     .rearrange("(n p) c -> p n c", p=128)).then_inc(x_ld[s].sem, 16)
            wait(sp, st, NTF, 0)
            for s in range(2):
                wait(sp, x_ld[s], NTF // 2, 2)

        @block.gpsimd
        def _(pool):
            n = 0
            for m, v in ((eps[:], EPS), (spread[:], 1.0)):
                nc.gpsimd.memset(m, v).then_inc(const, 1)
                n += 1
            for e in range(E):
                nc.gpsimd.memset(rank[:, :, e:e + 1], float(E - e)).then_inc(const, 1)
                n += 1
            for base_, step, sign in ((0, 1, -HE), (HE - 1, -1, HE)):
                pool.wait_ge(const, n)
                nc.gpsimd.affine_select(out=spread[:], in_=spread[:], compare_op=ALU.is_ge, fill=0.0, base=base_,
                                        pattern=[[step, E * HE]], channel_multiplier=sign).then_inc(const, 1)
                n += 1
            pool.wait_ge(const, n)

        NCONST = 2 + E + 2

        @block.vector
        def _(dve):
            tt = nc.vector.tensor_tensor
            for c in (hm, hw, ym):
                c.start(dve)
            dve.wait_ge(const, NCONST)
            dve.wait_ge(w_ld, 96)

            def normalize(t, s):
                i = t * 2 + s
                wait(dve, x_ld[s], t, 2)
                if s == 0:
                    wait(dve, ym, i, 0)
                else:
                    wait(dve, ym, i, 0)
                tt(x1[:], x[:, s], at[:, s], ALU.add).then_inc(x1m.sem, 1)
                bc = lambda v: v.unsqueeze(2).to_broadcast([128, NT, HID])
                mean, ssq, va = stat[:, 0:NT], stat[:, NT:2 * NT], stat[:, 2 * NT:3 * NT]
                wait(dve, x1m, i, 1)
                nc.vector.tensor_reduce(ssq, x1[:], AXIS.X, ALU.add).then_inc(ln.sem, 1)
                wait(dve, ln, i, 1)
                nc.vector.tensor_scalar(mean, ssq, 1.0 / HID, None, ALU.mult).then_inc(ln.sem, 1)
                wait(dve, ln, i, 2)
                tt(xc[:], x1[:], bc(mean), ALU.subtract).then_inc(ln.sem, 1)
                wait(dve, ln, i, 3)
                tt(xn[:], xc[:], xc[:], ALU.mult).then_inc(ln.sem, 1)
                wait(dve, ln, i, 4)
                nc.vector.tensor_reduce(ssq, xn[:], AXIS.X, ALU.add).then_inc(ln.sem, 1)
                wait(dve, ln, i, 5)
                nc.vector.tensor_scalar(va, ssq, 1.0 / HID, None, ALU.mult).then_inc(var.sem, 1)
                wait(dve, sd, i, 1)
                nc.vector.reciprocal(std[:, NT:2 * NT], std[:, 0:NT]).then_inc(ln.sem, 1)
                wait(dve, ln, i, 6)
                tt(xn[:], xc[:], bc(std[:, NT:2 * NT]), ALU.mult).then_inc(xnm.sem, 1)

            def route(i):
                wait(dve, sc, i, 1)
                n = [0]

                def step(ins):
                    n[0] += 1
                    ins.then_inc(rt.sem, 1)
                    wait(dve, rt, i, n[0])

                bc = lambda v: v.unsqueeze(2).to_broadcast([128, NT, E])
                step(tt(key[:], score[:], gbias[:].unsqueeze(1).to_broadcast([128, NT, E]), ALU.add))
                for k in range(TOPK):
                    step(nc.vector.tensor_reduce(best[:], key[:], AXIS.X, ALU.max))
                    step(tt(tmp[:], key[:], bc(best[:]), ALU.is_equal))
                    step(tt(tmp[:], tmp[:], rank[:], ALU.mult))
                    step(nc.vector.tensor_reduce(best[:], tmp[:], AXIS.X, ALU.max))
                    step(tt(tmp[:], rank[:], bc(best[:]), ALU.is_equal))
                    if k == 0:
                        step(nc.vector.tensor_copy(pick[:], tmp[:]))
                        step(nc.vector.tensor_scalar(tmp[:], tmp[:], -1e30, None, ALU.mult))
                        step(tt(key[:], key[:], tmp[:], ALU.add))
                    else:
                        step(tt(pick[:], pick[:], tmp[:], ALU.add))
                step(tt(wsel[:], score[:], pick[:], ALU.mult))
                step(nc.vector.tensor_reduce(best[:], wsel[:], AXIS.X, ALU.add))
                step(nc.vector.reciprocal(inv[:], best[:]))
                step(tt(wsel[:], wsel[:], bc(inv[:]), ALU.mult))
                assert n[0] == rt.per

            def tile(t, s):
                i = t * 2 + s
                normalize(t, s)
                for k, m in enumerate(order):
                    r = MROWS[m]
                    wait(dve, gs, i, k + 1)
                    tt(hid[0:r, m, :], act_g[0:r, k % 2, :], psU[k % 2][0:r, :], ALU.mult).then_inc(hm.sem, 1)
                    if m < ET:
                        wait(dve, wb, i, m + 1)
                        wait(dve, hm, i, k + 1)
                        tt(hid[:, m, :], hid[:, m, :], psW[m % 2][:], ALU.mult).then_inc(hw.sem, 1)
                    if k == 0:
                        route(i)
                for n in range(NT):
                    wait(dve, dn, i, n + 1)
                    wait(dve, st, i, 0)
                    tt(y[:, n, :], x1[:, n, :], psX[n % 2][:, 0:HID], ALU.add).then_inc(ym.sem, 1)

            with dve.Fori(0, NTF // 2) as t:
                tile(t, 0)
                tile(t, 1)

        @block.scalar
        def _(act):
            act.wait_ge(const, NCONST)

            def tile(t, s):
                i = t * 2 + s
                wait(act, var, i, 1)
                nc.scalar.activation(std[:, 0:NT], stat[:, 2 * NT:3 * NT], ACT.Sqrt, bias=eps[:, 0:1]).then_inc(sd.sem, 1)
                for kt in range(KT):
                    wait(act, xtp, i, kt + 1)
                    nc.scalar.activation(xT[:, kt, :], psX[kt][:], ACT.Copy).then_inc(xtm.sem, 1)
                wait(act, gp, i, 1)
                nc.scalar.activation(score[:].rearrange("p n e -> p (n e)"), psX[0][:, 0:NT * E], ACT.Sigmoid)\
                    .then_inc(sc.sem, 1)
                for k, m in enumerate(order):
                    if k == 3:
                        wait(act, wp, i, 1)
                        nc.scalar.activation(wT[:], psX[1][0:E, :], ACT.Copy).then_inc(wm.sem, 1)
                    r = MROWS[m]
                    wait(act, gu, i, k + 1)
                    wait(act, hm, i, k - 1)
                    nc.scalar.activation(act_g[0:r, k % 2, :], psG[k % 2][0:r, :], ACT.Silu).then_inc(gs.sem, 1)

            with act.Fori(0, NTF // 2) as t:
                tile(t, 0)
                tile(t, 1)

        @block.tensor
        def _(pe):
            mm = nc.tensor.matmul
            pe.wait_ge(w_ld, 96)
            pe.wait_ge(const, NCONST)

            def tile(t, s):
                i = t * 2 + s
                wait(pe, xnm, i, 1)
                wait(pe, ym, i, 0)
                for kt in range(KT):
                    for n in range(NT):
                        last = nc.tensor.transpose(psX[kt][:, 128 * n:128 * (n + 1)], xn[:, n, 128 * kt:128 * (kt + 1)], ident[:])
                    last.then_inc(xtp.sem, 1)
                wait(pe, xtm, i, 2)
                for n in range(NT):
                    for kt in range(KT):
                        last = mm(psX[0][:, E * n:E * (n + 1)], xT[:, kt, 128 * n:128 * (n + 1)], gate[:, kt, :],
                                  start=kt == 0, stop=kt == KT - 1)
                last.then_inc(gp.sem, 1)
                for k, m in enumerate(order):
                    r = MROWS[m]
                    if k == 3:
                        wait(pe, rt, i, ROUTE)
                        for n in range(NT):
                            last = nc.tensor.transpose(psX[1][0:E, 128 * n:128 * (n + 1)], wsel[:, n, :], ident[:])
                        last.then_inc(wp.sem, 1)
                        wait(pe, wm, i, 1)
                    wait(pe, hm, i, k - 1)
                    for ps, w in ((psG, wg), (psU, wu)):
                        for kt in range(KT):
                            last = mm(ps[k % 2][0:r, :], w[:, kt, 128 * m:128 * m + r], xT[:, kt, :],
                                      start=kt == 0, stop=kt == KT - 1)
                    last.then_inc(gu.sem, 1)
                    if m < ET:
                        wait(pe, hw, i, m - 1)
                        mm(psW[m % 2][:], spread[:, 128 * m:128 * (m + 1)], wT[:], start=True, stop=True).then_inc(wb.sem, 1)
                wait(pe, hm, i, MT)
                wait(pe, hw, i, ET)
                for n in range(NT):
                    wait(pe, ym, i, n - 1 if n >= 2 else 0)
                    for m in range(MT):
                        r = MROWS[m]
                        last = mm(psX[n % 2][:, 0:HID], hid[0:r, m, 128 * n:128 * (n + 1)], wd[0:r, m, :],
                                  start=m == 0, stop=m == MT - 1)
                    last.then_inc(dn.sem, 1)

            with pe.Fori(0, NTF // 2) as t:
                tile(t, 0)
                tile(t, 1)


def kernel(**inputs):
    import numpy as np
    import concourse.bacc as bacc
    from concourse.bass_utils import run_bass_kernel_spmd as run
    a = {k: np.asarray(v) for k, v in inputs.items()}
    n = lambda s: a["L0_attn_" + s]
    f = lambda s: a["L0_ffn_" + s]
    wp = np.stack([n(s).reshape(KT, 128, H, D).transpose(2, 1, 0, 3) for s in ("Wq", "Wk", "Wv", "Wa", "Wg")], 2)
    wp = wp.reshape(H, 128, WCOLS)
    cc = []
    for s in "qkv":
        cc += [n(s + "conv_w").reshape(H, D, TAPS), n(s + "conv_b").reshape(H, D, 1)]
    cc.append(n("ba").reshape(H, D, 1))
    wpack = np.concatenate([wp, *cc], 2)
    wpack = np.concatenate([wpack, np.zeros((2, *wpack.shape[1:]), np.float32)], 0)
    up = f("up_w")
    sg = f("shared_gw")
    wg = np.concatenate([up[:, :HE, :].reshape(E * HE, HID), sg[HS:]], 0).T
    wu = np.concatenate([up[:, HE:, :].reshape(E * HE, HID), sg[:HS]], 0).T
    wd = np.concatenate([f("down_w").transpose(0, 2, 1).reshape(E * HE, HID), f("shared_dw").T], 0)
    arrays = {
        "x": n("x").reshape(T, HID), "wb": n("Wb"), "bb": n("bb"), "wpack": wpack,
        "wo": n("Wo").reshape(H, D, HID).transpose(1, 0, 2), "ln_g": n("ln_g"), "ln_b": n("ln_b"),
        "gate": f("gate_w").T, "gate_bias": f("gate_bias"), "wg": wg, "wu": wu, "wd": wd,
    }
    arrays = {"in_" + k: np.ascontiguousarray(v) for k, v in arrays.items()}
    nc = bacc.Bacc("TRN2", target_bir_lowering=False, num_devices=1)
    args = {k: nc.dram_tensor(k, v.shape, mybir.dt.from_np(v.dtype), kind="ExternalInput").ap()
            for k, v in arrays.items()}
    out = nc.dram_tensor("out", (T, HID), FP32, kind="ExternalOutput").ap()
    build(nc, args, out)
    r = run(nc, [arrays], core_ids=[0])
    return r.results[0]["out"].reshape(1, T, HID)


def build(nc, a, out):
    scr = nc.dram_tensor("scr", (NPROJ, 128, H, T), FP32).ap()
    nbeta = nc.dram_tensor("nbeta", (H, T), FP32).ap()
    att = nc.dram_tensor("att", (T + 2 * C, HID), FP32).ap()
    ctx = ExitStack()
    with ctx:
        ident = ctx.enter_context(nc.sbuf_tensor("ident", [128, 128], FP32))
        made = ctx.enter_context(nc.semaphore("ident_made"))
        with nc.Block() as block:
            @block.gpsimd
            def _(pool):
                nc.gpsimd.memset(ident[:], 0.0).then_inc(made, 1)
                pool.wait_ge(made, 1)
                nc.gpsimd.affine_select(out=ident[:], in_=ident[:], compare_op=ALU.not_equal, fill=1.0, base=0,
                                        pattern=[[-1, 128]], channel_multiplier=1).then_inc(made, 1)
                pool.wait_ge(made, 2)
        project_inputs(nc, ident, a["in_x"], a["in_wb"], a["in_bb"], a["in_wpack"], scr, nbeta)
        recurrence(nc, ident, scr, nbeta, a["in_wo"], a["in_ln_g"], a["in_ln_b"], att)
        feed_forward(nc, ident, a["in_x"], att[2 * C:, :], a["in_gate"], a["in_gate_bias"],
                     a["in_wg"], a["in_wu"], a["in_wd"], out)
```

```python
import concourse.bass as bass
from concourse import mybir
from contextlib import ExitStack

FP32 = mybir.dt.float32
ALU = mybir.AluOpType
ACT = mybir.ActivationFunctionType
AXIS = mybir.AxisListType

T, HID = 2048, 256
H, D = 16, 128
TAPS = 4
E, TOPK = 8, 2
HE, HS = 176, 352
EPS = 1e-5
SCALE = float(D) ** -0.5
KT = HID // 128
TT = T // 128

TA = 512
NTA = T // TA
HALO = TAPS - 1
NPROJ = 5
Q_, K_, V_, A_, G_ = range(5)
WCOLS = NPROJ * KT * 128
CCOLS = 3 * (TAPS + 1) + 1

C = 64
R = 4
J = C // R
NCH = T // C
HC = H * C
HJ = H * J
LEVELS = [4, 8, 16, 32]
NC5 = R * (R + 1)

TF = 512
NTF = T // TF
HROWS = E * HE + HS
MT = -(-HROWS // 128)
MROWS = [min(128, HROWS - 128 * m) for m in range(MT)]
ET = E * HE // 128


class Count:

    def __init__(self, sem, per, unit=1, ahead=0):
        self.sem, self.per, self.unit, self.ahead = sem, per, unit, ahead

    def at(self, turn, k):
        return turn * (self.per * self.unit) + (self.ahead * self.per + k) * self.unit

    def start(self, eng):
        if self.ahead:
            eng.sem_inc(self.sem, self.ahead * self.per * self.unit)


def normalize_rows(nc, dve, act_wait, done, x, xc, sq, stat, n, base, signal_var):
    mean, ssq, var = stat[:, 0:n], stat[:, n:2 * n], stat[:, 2 * n:3 * n]
    bc = lambda s: s.unsqueeze(2).to_broadcast([128, n, HID])
    nc.vector.tensor_reduce(ssq, x, AXIS.X, ALU.add).then_inc(done, 1)
    dve.wait_ge(done, base + 1)
    nc.vector.tensor_scalar(mean, ssq, 1.0 / HID, None, ALU.mult).then_inc(done, 1)
    dve.wait_ge(done, base + 2)
    nc.vector.tensor_tensor(xc, x, bc(mean), ALU.subtract).then_inc(done, 1)
    dve.wait_ge(done, base + 3)
    nc.vector.tensor_tensor(sq, xc, xc, ALU.mult).then_inc(done, 1)
    dve.wait_ge(done, base + 4)
    nc.vector.tensor_reduce(ssq, sq, AXIS.X, ALU.add).then_inc(done, 1)
    dve.wait_ge(done, base + 5)
    nc.vector.tensor_scalar(var, ssq, 1.0 / HID, None, ALU.mult).then_inc(signal_var, 1)


def project_inputs(nc, ident, x_d, wb_d, bb_d, wpack_d, scr, nbeta_d):
    ctx = ExitStack()
    with ctx:
        sb = lambda name, shape: ctx.enter_context(nc.sbuf_tensor(name, shape, FP32))
        sem = lambda name: ctx.enter_context(nc.semaphore(name))
        x = sb("A_x", [128, TT, HID])
        xc = sb("A_xc", [128, TT, HID])
        xn = sb("A_xn", [128, TT, HID])
        stat = sb("A_stat", [128, 3 * TT])
        std = sb("A_std", [128, 2 * TT])
        eps = sb("A_eps", [128, 1])
        xT = sb("A_xT", [128, KT, HALO + T])
        factors = sb("A_factors", [128, 2])
        wb = sb("A_wb", [128, KT, H])
        bb = sb("A_bb", [H, 1])
        beta = sb("A_beta", [H, T])
        nbeta = sb("A_nbeta", [H, T])
        w = sb("A_w", [128, 2, WCOLS + CCOLS])
        acc = sb("A_acc", [128, 3, 2, TA])
        outs = sb("A_outs", [128, 2, 3, T])
        outag = sb("A_outag", [128, 2, 2, T])
        psY = [ctx.enter_context(nc.psum_tensor(f"A_psY{i}", [128, 2 * 512], FP32)) for i in range(3)]
        psAG = [ctx.enter_context(nc.psum_tensor(f"A_psAG{i}", [128, 512], FP32)) for i in range(2)]
        loaded, const_ld = sem("A_x_loaded"), sem("A_const_loaded")
        ln_step, var_done, std_done, xn_done = sem("A_ln_step"), sem("A_var"), sem("A_std"), sem("A_xn")
        pads, xT_ps, xT_a, xT_v = sem("A_pads"), sem("A_xT_ps"), sem("A_xT_act"), sem("A_xT_dve")
        beta_ps, beta_sb, nbeta_sb, nbeta_st = sem("A_beta_ps"), sem("A_beta"), sem("A_nbeta"), sem("A_nbeta_st")
        TURNS = H // 2
        w_ld = [Count(sem(f"A_w_ld{s}"), 1, 16) for s in range(2)]
        w_used = [Count(sem(f"A_w_used{s}"), 1, 1, 1) for s in range(2)]
        c_used = [Count(sem(f"A_c_used{s}"), 1, 1, 1) for s in range(2)]
        ca_used = [Count(sem(f"A_ca_used{s}"), 1, 1, 1) for s in range(2)]
        y_full = [Count(sem(f"A_y_full{p}"), 2 * NTA) for p in range(3)]
        ag_full = [Count(sem(f"A_ag_full{p}"), 2 * NTA) for p in range(2)]
        ag_free = [Count(sem(f"A_ag_free{p}"), 2 * NTA, 1, 1) for p in range(2)]
        acc_set = [Count(sem(f"A_acc_set{p}"), 2 * NTA) for p in range(3)]
        tap = [Count(sem(f"A_tap{p}"), 2 * NTA * 3, 1, 1) for p in range(3)]
        sig = [Count(sem(f"A_sig{p}"), 2 * NTA) for p in range(3)]
        silu = [Count(sem(f"A_silu{p}"), 2 * NTA, 1, 1) for p in range(3)]
        scaled = [Count(sem(f"A_scaled{p}"), 2, 1, 1) for p in (K_, V_)]
        st_qkv = [Count(sem(f"A_st_qkv{s}"), 3, 16, 1) for s in range(2)]
        st_ag = [Count(sem(f"A_st_ag{s}"), 2, 16, 1) for s in range(2)]

        block = ctx.enter_context(nc.Block())

        @block.sync
        def _(sp):
            for i in range(4):
                n = TT // 4
                sp.dma_start(x[:, i * n:(i + 1) * n, :],
                             x_d.rearrange("(n p) c -> p n c", p=128)[:, i * n:(i + 1) * n, :]).then_inc(loaded, 16)
            sp.dma_start(wb[:], wb_d.rearrange("(k p) h -> p k h", p=128)).then_inc(const_ld, 16)
            sp.dma_start(bb[:], bb_d.rearrange("(h o) -> h o", o=1)).then_inc(const_ld, 16)
            for c in (*st_qkv, *st_ag):
                c.start(sp)
            for s in range(2):
                sp.dma_start(w[:, s, :], wpack_d[s]).then_inc(w_ld[s].sem, 16)
            sp.wait_ge(nbeta_sb, 1)
            sp.dma_start(nbeta_d, nbeta[:]).then_inc(nbeta_st, 16)
            with sp.Fori(0, TURNS) as t:
                for s in range(2):
                    head = scr[:, :, bass.ds(t * 2 + s, 1), :]
                    sp.wait_ge(silu[Q_].sem, silu[Q_].at(t, (s + 1) * NTA))
                    sp.dma_start(head[Q_], outs[:, s, Q_, :].unsqueeze(1)).then_inc(st_qkv[s].sem, 16)
                    for p in range(2):
                        sp.wait_ge(ag_free[p].sem, ag_free[p].at(t, (s + 1) * NTA))
                        sp.dma_start(head[A_ + p], outag[:, s, p, :].unsqueeze(1)).then_inc(st_ag[s].sem, 16)
                    sp.wait_ge(scaled[0].sem, scaled[0].at(t, s + 1))
                    sp.dma_start(head[K_], outs[:, s, K_, :].unsqueeze(1)).then_inc(st_qkv[s].sem, 16)
                    sp.wait_ge(scaled[1].sem, scaled[1].at(t, s + 1))
                    sp.dma_start(head[V_], outs[:, s, V_, :].unsqueeze(1)).then_inc(st_qkv[s].sem, 16)
                    sp.wait_ge(w_used[s].sem, w_used[s].at(t, 1))
                    sp.wait_ge(c_used[s].sem, c_used[s].at(t, 1))
                    sp.wait_ge(ca_used[s].sem, ca_used[s].at(t, 1))
                    sp.dma_start(w[:, s, :], wpack_d[bass.ds(t * 2 + (s + 2), 1)].rearrange("o p c -> p (o c)"))\
                      .then_inc(w_ld[s].sem, 16)
            for s in range(2):
                sp.wait_ge(st_qkv[s].sem, st_qkv[s].at(TURNS, 0))
                sp.wait_ge(w_ld[s].sem, w_ld[s].at(TURNS, 1))
                sp.wait_ge(st_ag[s].sem, st_ag[s].at(TURNS, 0))
            sp.wait_ge(nbeta_st, 16)

        @block.gpsimd
        def _(pool):
            nc.gpsimd.memset(xT[:, :, 0:HALO], 0.0).then_inc(pads, 1)
            nc.gpsimd.memset(eps[:], EPS).then_inc(pads, 1)
            nc.gpsimd.memset(factors[:, 0:1], SCALE).then_inc(pads, 1)
            nc.gpsimd.memset(factors[:, 1:2], -1.0).then_inc(pads, 1)
            pool.wait_ge(pads, 4)
            for c in (*scaled, *silu):
                c.start(pool)
            with pool.Fori(0, TURNS) as t:
                for s in range(2):
                    for i in range(NTA):
                        n = s * NTA + i
                        for p in range(3):
                            pool.wait_ge(sig[p].sem, sig[p].at(t, n + 1))
                            o = outs[:, s, p, TA * i:TA * (i + 1)]
                            nc.gpsimd.tensor_tensor(o, o, acc[:, p, n % 2, :], ALU.mult).then_inc(silu[p].sem, 1)
                    for i, (p, factor) in enumerate(((K_, SCALE), (V_, -1.0))):
                        pool.wait_ge(silu[p].sem, silu[p].at(t, (s + 1) * NTA))
                        o = outs[:, s, p, :]
                        nc.gpsimd.tensor_tensor(o, o, factors[:, i:i + 1].to_broadcast([128, T]), ALU.mult)\
                          .then_inc(scaled[i].sem, 1)

        @block.vector
        def _(dve):
            dve.wait_ge(loaded, 64)
            normalize_rows(nc, dve, None, ln_step, x[:], xc[:], xn[:], stat, TT, 0, var_done)
            dve.wait_ge(std_done, 1)
            nc.vector.reciprocal(std[:, TT:2 * TT], std[:, 0:TT]).then_inc(ln_step, 1)
            dve.wait_ge(ln_step, 6)
            dve.wait_ge(var_done, 1)
            nc.vector.tensor_tensor(xn[:], xc[:], std[:, TT:2 * TT].unsqueeze(2).to_broadcast([128, TT, HID]),
                                    ALU.mult).then_inc(xn_done, 1)
            for g in range(4):
                dve.wait_ge(xT_ps, 5 + g)
                src = (psY[2][:, 0:512], psY[2][:, 512:1024], psAG[0][:], psAG[1][:])[g]
                nc.vector.tensor_copy(xT[:, 1, HALO + 512 * g:HALO + 512 * (g + 1)], src).then_inc(xT_v, 1)
            for p in range(3):
                tap[p].start(dve)
            c_used[0].start(dve)
            c_used[1].start(dve)
            with dve.Fori(0, TURNS) as t:
                for s in range(2):
                    dve.wait_ge(w_ld[s].sem, w_ld[s].at(t, 1))
                    for i in range(NTA):
                        n = s * NTA + i
                        for k in range(3):
                            for p in range(3):
                                if k == 0:
                                    dve.wait_ge(acc_set[p].sem, acc_set[p].at(t, n + 1))
                                else:
                                    dve.wait_ge(tap[p].sem, tap[p].at(t, 3 * n + k))
                                a = acc[:, p, n % 2, :].rearrange("p (b c) -> p b c", b=2)
                                j = TAPS - 2 - k
                                y = psY[p][:, :].rearrange("p (b c) -> p b c", b=2)[:, :, j:j + TA // 2]
                                col = WCOLS + p * (TAPS + 1) + j
                                nc.vector.scalar_tensor_tensor(a, y, w[:, s, col:col + 1], a, ALU.mult, ALU.add)\
                                  .then_inc(tap[p].sem, 1)
                    dve.wait_ge(tap[2].sem, tap[2].at(t, 3 * (s + 1) * NTA))
                    dve.sem_inc(c_used[s].sem, 1)

        @block.scalar
        def _(act):
            act.wait_ge(pads, 4)
            act.wait_ge(var_done, 1)
            nc.scalar.activation(std[:, 0:TT], stat[:, 2 * TT:3 * TT], ACT.Sqrt, bias=eps[:, 0:1]).then_inc(std_done, 1)
            for g in range(4):
                act.wait_ge(xT_ps, g + 1)
                nc.scalar.activation(xT[:, 0, HALO + 512 * g:HALO + 512 * (g + 1)],
                                     psY[g // 2][:, 512 * (g % 2):512 * (g % 2 + 1)], ACT.Copy).then_inc(xT_a, 1)
            act.wait_ge(const_ld, 32)
            for g in range(NTA):
                act.wait_ge(beta_ps, g + 1)
                nc.scalar.activation(beta[:, 512 * g:512 * (g + 1)], psY[g // 2][0:H, 512 * (g % 2):512 * (g % 2 + 1)],
                                     ACT.Sigmoid, bias=bb[:, 0:1]).then_inc(beta_sb, 1)
            act.wait_ge(beta_sb, NTA)
            nc.scalar.activation(nbeta[:], beta[:], ACT.Copy, scale=-1.0).then_inc(nbeta_sb, 1)
            for c in (*ag_free, *ca_used):
                c.start(act)

            with act.Fori(0, TURNS) as t:
                for s in range(2):
                    act.wait_ge(w_ld[s].sem, w_ld[s].at(t, 1))
                    act.wait_ge(st_qkv[s].sem, st_qkv[s].at(t, 0))
                    for i in range(NTA + 1):
                        if i < NTA:
                            n = s * NTA + i
                            for p in range(3):
                                act.wait_ge(y_full[p].sem, y_full[p].at(t, n + 1))
                                col = WCOLS + p * (TAPS + 1)
                                act.wait_ge(silu[p].sem, silu[p].at(t, n - 1))
                                nc.scalar.activation(
                                    acc[:, p, n % 2, :].rearrange("p (b c) -> p b c", b=2),
                                    psY[p][:, :].rearrange("p (b c) -> p b c", b=2)[:, :, HALO:HALO + TA // 2],
                                    ACT.Identity, scale=w[:, s, col + HALO:col + HALO + 1],
                                    bias=w[:, s, col + TAPS:col + TAPS + 1]).then_inc(acc_set[p].sem, 1)
                        if i > 0:
                            n = s * NTA + i - 1
                            for p in range(3):
                                act.wait_ge(tap[p].sem, tap[p].at(t, 3 * (n + 1)))
                                nc.scalar.activation(outs[:, s, p, TA * (i - 1):TA * i], acc[:, p, n % 2, :], ACT.Sigmoid)\
                                  .then_inc(sig[p].sem, 1)
                        if i == NTA:
                            continue
                        if i == 0:
                            act.wait_ge(st_ag[s].sem, st_ag[s].at(t, 0))
                        for p in range(2):
                            act.wait_ge(ag_full[p].sem, ag_full[p].at(t, s * NTA + i + 1))
                            bias = w[:, s, WCOLS + CCOLS - 1:WCOLS + CCOLS] if p == 0 else 0.0
                            nc.scalar.activation(outag[:, s, p, TA * i:TA * (i + 1)], psAG[p][:], ACT.Sigmoid, bias=bias)\
                              .then_inc(ag_free[p].sem, 1)
                    act.wait_ge(ag_free[0].sem, ag_free[0].at(t, (s + 1) * NTA))
                    act.sem_inc(ca_used[s].sem, 1)

        @block.tensor
        def _(pe):
            pe.wait_ge(xn_done, 1)
            for kt in range(KT):
                for g in range(4):
                    n = kt * 4 + g
                    ps = psY[n // 2][:, 512 * (n % 2):512 * (n % 2 + 1)] if n < 6 else psAG[n - 6][:]
                    for m in range(4):
                        last = nc.tensor.transpose(ps[:, 128 * m:128 * (m + 1)],
                                                   xn[:, 4 * g + m, 128 * kt:128 * (kt + 1)], ident[:])
                    last.then_inc(xT_ps, 1)
            pe.wait_ge(pads, 1)
            pe.wait_ge(xT_a, 4)
            pe.wait_ge(xT_v, 4)
            pe.wait_ge(const_ld, 32)
            for g in range(NTA):
                for kt in range(KT):
                    last = nc.tensor.matmul(psY[g // 2][0:H, 512 * (g % 2):512 * (g % 2 + 1)], wb[:, kt, :],
                                            xT[:, kt, HALO + 512 * g:HALO + 512 * (g + 1)],
                                            start=kt == 0, stop=kt == KT - 1)
                last.then_inc(beta_ps, 1)
            pe.wait_ge(beta_sb, NTA)
            w_used[0].start(pe)
            w_used[1].start(pe)
            with pe.Fori(0, TURNS) as t:
                for s in range(2):
                    pe.wait_ge(w_ld[s].sem, w_ld[s].at(t, 1))
                    wp = w[:, s, 0:WCOLS].rearrange("p (j k c) -> p j k c", j=NPROJ, k=KT)
                    for i in range(NTA):
                        n = s * NTA + i
                        for p in range(3):
                            pe.wait_ge(tap[p].sem, tap[p].at(t, 3 * n))
                            for kt in range(KT):
                                for b in range(2):
                                    t0 = i * TA + b * (TA // 2)
                                    last = nc.tensor.matmul(psY[p][:, 512 * b:512 * b + HALO + TA // 2], wp[:, p, kt, :],
                                                            xT[:, kt, t0:t0 + HALO + TA // 2],
                                                            start=kt == 0, stop=kt == KT - 1)
                            last.then_inc(y_full[p].sem, 1)
                        for p in range(2):
                            pe.wait_ge(ag_free[p].sem, ag_free[p].at(t, n))
                            for kt in range(KT):
                                last = nc.tensor.matmul(psAG[p][:], wp[:, A_ + p, kt, :],
                                                        xT[:, kt, HALO + i * TA:HALO + (i + 1) * TA],
                                                        start=kt == 0, stop=kt == KT - 1)
                            last.then_inc(ag_full[p].sem, 1)
                    pe.wait_ge(ag_full[1].sem, ag_full[1].at(t, (s + 1) * NTA))
                    pe.sem_inc(w_used[s].sem, 1)


def leaf_jobs(s, j):
    return {0: [("mean", 0)], 1: [("mean", 1)], 2: [("gram", 2), ("kk", 1, 0)], 3: [("kk", 1, 1), ("gram", 3)],
            4: [("var", 0), ("gram", 4)], 5: [("qk", 0, 0), ("qk", 0, 2)], 6: [("qk", 0, 1), ("rstd", 0)],
            7: [("rstd", 1), ("gram", 5)], 8: [("gram", 6), ("decay", 0)], 9: [("decay", 1), ("decay", 2)],
            10: [("gram", 7)] + ([("wo", 0)] if s == 1 else []), 11: [("decay", 3), ("ktok", 0), ("ktok", 1)],
            12: [("kk", 0, 0)], 13: [("kk", 0, 1), ("gram", 0)], 14: [("qk", 1, 0)],
            15: [("qk", 1, 1), ("qk", 1, 2)]}.get(j, [])


def turn_jobs():
    out = []
    for s in range(2):
        out += [(s, "contact", i) for i in range(4)]
        for j in range(J):
            out += [(s, *x) for x in leaf_jobs(s, j)]
        out += [(s, "wtok", i) for i in range(2)] + [(s, "gram", 1)] + [(s, "update", i) for i in range(4)]
    return out


PROLOGUE = [("first", "kk", 0, 0), ("first", "kk", 0, 1)] + [("first", "gram", i) for i in range(2)]
NORM = [("mean", 0), ("mean", 1), ("var", 0), ("rstd", 0), ("rstd", 1)]
EPILOGUE = ([("last", *x) for x in NORM] + [("last", "qk", h, i) for h in range(2) for i in range(3)]
            + [("end", *x) for x in NORM] + [("end", "wo", 0)])
RING = 5
PAIRS = 6
NCS = 15
DEC = 6


def merge_of(j):
    p = 0
    while (j >> p) & 1:
        p += 1
    return p, R << p, R * (j + 1)


def pair_number(j):
    return j // 2


def gram_places():
    out, n = {}, 0
    for half in range(2):
        js = [j for j in range(8 * half, 8 * half + 8) if j < J - 1]
        for p in range(4):
            tiles = [(j, i) for j in js if merge_of(j)[0] == p for i in range(1 if p == 0 else 1 << (p - 1))]
            width = 128 if p == 0 else 256
            for k, x in enumerate(tiles):
                out[x] = (n + k * width // 512, k * width % 512)
            n += -(-len(tiles) * width // 512)
    return out


def recurrence(nc, ident, scr, nbeta_d, wo_d, lng_d, lnb_d, att_d):
    ctx = ExitStack()
    with ctx:
        sb = lambda name, shape: ctx.enter_context(nc.sbuf_tensor("B_" + name, shape, FP32))
        sem = lambda name: ctx.enter_context(nc.semaphore("B_" + name))
        wo = sb("wo", [128, H, HID])
        lng, lnb, eps = sb("lng", [128, 1]), sb("lnb", [128, 1]), sb("eps", [128, 1])
        ones, avg = sb("ones", [128, 128]), sb("avg", [128, 128])
        masks = sb("masks", [128, 4, 128])
        KQ = sb("KQ", [128, 2, 2, H, C])
        NV, A, G, NB = [sb(x, [128, 2, H, C]) for x in ("NV", "A", "G", "NB")]
        A2 = sb("A2", [128, H, C])
        HC2 = C // 2
        HJ2 = H * J // 2
        KB = sb("KB", [128, H, HC2])
        X = sb("X", [128, PAIRS, HJ2])
        Y = sb("Y", [128, 4 + PAIRS, HJ2])
        RR = sb("RR", [128, 2, H, J])
        F, B = sb("F", [128, 2, H, C]), sb("B", [128, H, C])
        Gs = [sb(f"G{i}", [128, H, J >> i]) for i in range(5)]
        NC = sb("NC", [128, 2, H, J // 2, R * (R + 1)])
        TMP = sb("TMP", [128, H, J // 2, 6])
        ST = sb("ST", [128, H, 128])
        P, Q = sb("P", [128, H, C]), sb("Q", [128, 2, H, C])
        W = sb("W", [128, 2, H, C])
        WT = sb("WT", [128, J, H, R])
        WE = sb("WE", [128, H, C])
        WC = WE[:].rearrange("p h c -> p (h c)")
        KL = sb("KL", [128, J // 2, H, R])
        KC = sb("KC", [128, 3, 256])
        BD = sb("BD", [128, 8, 512])
        KTOK, WTOK = sb("KTOK", [128, 8, 128]), sb("WTOK", [128, 8, 128])
        WL = sb("WL", [128, 512])
        AW = sb("AW", [128, 3, HJ2])
        O, SQ = sb("O", [128, H, C]), sb("SQ", [128, H, C])
        sdev, rdev = sb("sdev", [128, 8]), sb("rdev", [128, 8])
        OG = sb("OG", [128, H, 2 * C])
        att = sb("att", [128, HID])
        ring = [ctx.enter_context(nc.psum_tensor(f"B_ring{i}", [128, 512], FP32)) for i in range(RING)]
        psT = ctx.enter_context(nc.psum_tensor("B_psT", [128, 512], FP32))
        psM = ctx.enter_context(nc.psum_tensor("B_psM", [128, 1024], FP32))

        TURNS = NCH // 2
        JM = J - 1
        grams = gram_places()
        place = {}
        counts = []
        for part in (PROLOGUE, turn_jobs(), EPILOGUE):
            seen = [0] * RING
            for n, job in enumerate(part):
                place[job] = (n % RING, seen[n % RING])
                seen[n % RING] += 1
            counts.append(seen)
        base, per = counts[0], counts[1]
        full = [Count(sem(f"bank{b}_full"), per[b], 1, 0) for b in range(RING)]
        cl, wol = Count(sem("const_ld"), 2, 16), Count(sem("wo_ld"), 1, 16)
        const, zeros = Count(sem("const"), 32), Count(sem("zeros"), 7)
        cst = Count(sem("state_zero"), 1)
        ld = {x: [Count(sem(f"ld_{x}{s}"), 1, 16) for s in range(2)] for x in ("K", "Q", "NV", "A", "G", "NB")}
        kb, xm = Count(sem("kb"), 1), Count(sem("x_made"), 3)
        dec, dcp = Count(sem("decays"), DEC), Count(sem("decay_copies"), 2)
        gb, nc0 = Count(sem("block_decays"), 3), Count(sem("leaf_diagonals"), 2)
        g4 = Count(sem("g4"), 1)
        nl, nlc = Count(sem("nl"), 2), Count(sem("nl_copy"), 1)
        ncs = Count(sem("leaf_solutions"), NCS)
        bd, bda = Count(sem("grams_masked"), 6), Count(sem("grams_masked_act"), 2)
        ktok, wtok = Count(sem("ktok"), 2, 1, 1), Count(sem("wtok"), 2)
        cont = Count(sem("contact_copied"), 8)
        ap = Count(sem("leaf_terms"), J)
        ws = Count(sem("w_solved"), J, 1, 1)
        wt = Count(sem("w_decayed"), J)
        psc, psc0 = Count(sem("pq_scaled"), JM - 1), Count(sem("leaf_pq_scaled"), JM + 1)
        wsc, wsc0 = Count(sem("w_scaled"), JM // 2, 1, 1), Count(sem("leaf_w_scaled"), JM // 2 + 1, 1, 1)
        tps = Count(sem("left_ps"), JM)
        wl = Count(sem("left_copied"), JM, 1, 1)
        kc = Count(sem("k_compact"), 5)
        wc = Count(sem("left_compact"), 3)
        wec = Count(sem("w_end"), 2)
        mps = Count(sem("merge_ps"), 2 * JM, 1, 1)
        mg = Count(sem("merged"), 2 * JM, 1, 1)
        stg, stu = Count(sem("state_decayed"), 4), Count(sem("state_updated"), 4, 1, 1)
        a2 = Count(sem("a2_copied"), 1, 1, 0)
        ym = Count(sem("y_made"), 8, 1, 1)
        awm = Count(sem("aw_made"), 4)
        yv = Count(sem("y_terms"), 8)
        om = Count(sem("o_made"), 12)
        oc, sqd = Count(sem("o_centered"), 2), Count(sem("o_squared"), 1)
        sd, rd = Count(sem("sdev"), 1), Count(sem("rdev"), 1)
        on, aff = Count(sem("o_normed"), 2), Count(sem("o_affine"), 1)
        og = Count(sem("o_gated"), 1, 1, 1)
        am, ast = Count(sem("att_made"), 1), Count(sem("att_st"), 1, 16, 1)

        def wait(eng, c, index, k):
            eng.wait_ge(c.sem, c.at(index, k))

        def loaded(eng, what, t, c):
            wait(eng, ld[what][c % 2], t + c // 2, 1)

        def masked(n):
            return (bda, n - 2) if n in (3, 4) else (bd, n + 1 if n < 3 else n - 1)

        def taken(t, label, job):
            kind, n = job[0], job[-1]
            if label == "first":
                return (bd, 0, n + 1) if kind == "gram" else ((nl, 0, 2) if n else (nlc, 0, 1))
            g = NCH if label == "last" else NCH + 1 if label == "end" else t * 2 + label
            if kind == "kk":
                i = g * 2 + (1 if job[1] else 2)
                return (nl, i, 2) if n else (nlc, i, 1)
            if kind == "gram":
                return masked(n)[0], g + (n < 2), masked(n)[1]
            if kind == "qk":
                return yv, g, 4 * job[1] + (1, 3, 4)[n]
            if kind == "wo":
                return am, t, 1
            return {"contact": (cont, g, n + 5), "ktok": (ktok, g, n + 1), "decay": (stg, g, n + 1), "mean": (oc, g, n + 1),
                    "var": (sd, g, 1), "rstd": (on, g, n + 1), "wtok": (wtok, g, n + 1), "update": (stu, g, n + 1)}[kind]

        parts = {"first": PROLOGUE, "last": EPILOGUE, "end": EPILOGUE}

        def open_bank(pe, t, label, *job):
            part = parts.get(label, turn_jobs())
            n = part.index((label, *job))
            if n >= RING:
                before, tb = part[n - RING], t
            elif label == "first":
                before = None
            elif label in ("last", "end") or not (isinstance(t, int) and t == 0):
                before, tb = [x for m, x in enumerate(turn_jobs()) if m % RING == n][-1], t - 1
            else:
                before, tb = ([None] + [x for m, x in enumerate(PROLOGUE) if m % RING == n])[-1], 0
            if before:
                c, i, k = taken(tb, before[0], before[1:])
                wait(pe, c, i, k)
            b = n % RING
            return ring[b], full[b].sem

        def take_bank(eng, t, label, *job):
            b, k = place[(label, *job)]
            v = k + 1 if label == "first" else (TURNS if label in ("last", "end") else t) * per[b] + base[b] + k + 1
            eng.wait_ge(full[b].sem, v)
            return ring[b]

        YV = SQ[:].rearrange("p h c -> p (h c)")[:, 0:7 * HJ2].rearrange("p (n h j) -> p n h j", n=7, h=H)

        def leafwise(ap, h):
            return ap[:, :, HC2 * h:HC2 * (h + 1)].rearrange("p h (j r) -> p r h j", r=R)

        def rows(ap):
            return ap.rearrange("p n (h j) -> p n h j", h=H)

        block = ctx.enter_context(nc.Block())

        @block.sync
        def _(sp):
            sp.dma_start(lng[:], lng_d.rearrange("(p o) -> p o", o=1)).then_inc(cl.sem, 16)
            sp.dma_start(lnb[:], lnb_d.rearrange("(p o) -> p o", o=1)).then_inc(cl.sem, 16)
            ast.start(sp)

            def load(what, s, at):
                dst = {"K": KQ[:, s, 0], "Q": KQ[:, s, 1], "NV": NV[:, s], "A": A[:, s], "G": G[:, s], "NB": NB[:, s]}[what]
                n = {"K": K_, "Q": Q_, "NV": V_, "A": A_, "G": G_}
                src = nbeta_d[:, bass.ds(at, C)].partition_broadcast(128) if what == "NB" else scr[n[what]][:, :, bass.ds(at, C)]
                sp.dma_start(dst, src).then_inc(ld[what][s].sem, 16)

            sp.wait_ge(const.sem, 32)
            wait(sp, zeros, 0, 7)
            for what in ("A", "K", "NB", "Q", "NV"):
                load(what, 0, 0)
            sp.dma_start(wo[:], wo_d).then_inc(wol.sem, 16)

            def chunk(t, s, here, at):
                n = (s + 1) % 2
                g = t * 2 + s
                wait(sp, ncs, t * 4 + 2 * s, 0) if not (isinstance(t, int) and t == 0 and s == 0) else None
                load("NV", n, at)
                load("NB", n, at)
                wait(sp, a2, g, 1)
                load("A", n, at)
                wait(sp, ym, g, 8)
                load("K", n, at)
                load("Q", n, at)
                wait(sp, og, g, 1)
                load("G", s, here)
                if s == 1:
                    wait(sp, am, t, 1)
                    sp.dma_start(att_d[bass.ds(t * (2 * C), 2 * C), :], att[:]).then_inc(ast.sem, 16)

            chunk(0, 0, 0, C)
            chunk(0, 1, C, 2 * C)
            with sp.Fori(1, TURNS - 1) as t:
                chunk(t, 0, t * (2 * C), t * (2 * C) + C)
                chunk(t, 1, t * (2 * C) + C, t * (2 * C) + 2 * C)
            chunk(TURNS - 1, 0, T - 2 * C, T - C)
            chunk(TURNS - 1, 1, T - C, 0)
            wait(sp, am, TURNS, 1)
            sp.dma_start(att_d[TURNS * 2 * C:(TURNS + 1) * 2 * C, :], att[:]).then_inc(ast.sem, 16)
            wait(sp, ast, TURNS, 1)
            for what in ("K", "NB", "NV", "A", "Q"):
                loaded(sp, what, TURNS, 0)

        @block.gpsimd
        def _(pool):
            tt = nc.gpsimd.tensor_tensor
            nconst = 0
            for ap_, v in ((WT[:], 0.0), (ones[:], 1.0), (avg[:], 1.0 / D), (eps[:], EPS), (A[:, 1], 0.0),
                          (W[:, 1], 0.0), (RR[:, 1], 0.0), (F[:, 1], 1.0), (F[:, 0], 1.0), (B[:], 1.0), (masks[:], 1.0)):
                nc.gpsimd.memset(ap_, v).then_inc(const.sem, 1)
                nconst += 1
            for p in range(4):
                n = 64 if p == 0 else 128
                w_ = R << p
                rw, nr = (R, 2) if p == 1 else (w_, 1)
                for r0 in range(0, n, n // nr):
                    m = masks[r0:r0 + n // nr, p, 0:n].rearrange("p (h t) -> p h t", t=w_)
                    for base_, step, sign in ((0, -rw, 1), (rw - 1, rw, -1)):
                        pool.wait_ge(const.sem, nconst)
                        nc.gpsimd.affine_select(out=m, in_=m, compare_op=ALU.is_ge, fill=0.0, base=base_,
                                                pattern=[[step, n // w_], [0, w_]], channel_multiplier=sign)\
                          .then_inc(const.sem, 1)
                        nconst += 1
            while nconst < 32:
                pool.wait_ge(const.sem, nconst)
                nc.gpsimd.memset(TMP[:, 0:1, 0:1], 0.0).then_inc(const.sem, 1)
                nconst += 1
            wait(pool, zeros, 0, 7)
            for c in (wsc, ym, og):
                c.start(pool)

            def half(t, c4):
                return t * 4 + c4

            def products_kk(t, c4, part):
                s, h, g = c4 // 2 % 2, c4 % 2, t * 2 + c4 // 2
                kx = KQ[:, s, 0][:, :, HC2 * h:HC2 * (h + 1)]
                kr, br, xr = leafwise(KQ[:, s, 0], h), KB[:].rearrange("p h (j r) -> p r h j", r=R), rows(X[:])
                if part == 0:
                    loaded(pool, "K", t, c4 // 2)
                    loaded(pool, "NB", t, c4 // 2)
                    if not (isinstance(t, int) and t == 0 and c4 == 0):
                        wait(pool, xm, half(t, c4), 0)
                    tt(KB[:], kx, NB[:, s, :, HC2 * h:HC2 * (h + 1)], ALU.mult).then_inc(kb.sem, 1)
                elif part == 1:
                    wait(pool, kb, half(t, c4), 1)
                    if not (isinstance(t, int) and t == 0 and c4 == 0):
                        wait(pool, ncs, half(t, c4), 0)
                    tt(xr[:, 0:3], br[:, 1:4], kr[:, 0:3], ALU.mult).then_inc(xm.sem, 1)
                elif part == 2:
                    tt(xr[:, 3], br[:, 3], kr[:, 0], ALU.mult).then_inc(xm.sem, 1)
                else:
                    tt(xr[:, 4:6], br[:, 2:4], kr[:, 0:2], ALU.mult).then_inc(xm.sem, 1)

            def block_decays(t, c4):
                h, g, i = c4 % 2, t * 2 + c4 // 2, half(t, c4)
                wait(pool, dec, i, DEC)
                if not (isinstance(t, int) and t == 0 and c4 < 2):
                    wait(pool, psc, g - 1, 14 if h else 8)
                    wait(pool, wsc, g - 1, 7 if h else 3)
                for p in (1, 2, 3):
                    if p > 1:
                        wait(pool, gb, i, p - 1)
                    n = J >> p
                    lo = Gs[p - 1][:, :, n * h:n * (h + 1)].rearrange("p h (j two) -> p two h j", two=2)
                    tt(Gs[p][:, :, n // 2 * h:n // 2 * (h + 1)], lo[:, 0], lo[:, 1], ALU.mult).then_inc(gb.sem, 1)
                if h == 1:
                    wait(pool, gb, i, 3)
                    if not (isinstance(t, int) and t == 0 and c4 == 1):
                        wait(pool, stg, g, 0)
                    tt(Gs[4][:], Gs[3][:, :, 0:1], Gs[3][:, :, 1:2], ALU.mult).then_inc(g4.sem, 1)

            def leaf_diagonals(t, c4):
                s, h, g, i = c4 // 2 % 2, c4 % 2, t * 2 + c4 // 2, half(t, c4)
                n, x = NC[:, h], slice(HC2 * h, HC2 * (h + 1))
                by_leaf = lambda ap: ap.rearrange("p h (j r) -> p h j r", r=R)
                wait(pool, dec, i, DEC)
                loaded(pool, "NB", t, c4 // 2)
                loaded(pool, "NV", t, c4 // 2)
                if not (isinstance(t, int) and t == 0 and c4 < 2):
                    wait(pool, ws, g - 1, 8 * h + 8)
                tt(n[:, :, :, 1::6], by_leaf(NB[:, s, :, x]), by_leaf(F[:, s, :, x]), ALU.mult).then_inc(nc0.sem, 1)
                tt(n[:, :, :, 0::5], by_leaf(NB[:, s, :, x]), by_leaf(NV[:, s, :, x]), ALU.mult).then_inc(nc0.sem, 1)

            def products_qk(t, g, label, s, h, part):
                kr, qr, yr = leafwise(KQ[:, s, 0], h), leafwise(KQ[:, s, 1], h), rows(Y[:])
                if part == 0:
                    for i in range(3):
                        if h == 1:
                            take_bank(pool, t, label, "qk", 0, i)
                        elif label == 1:
                            take_bank(pool, t, 0, "qk", 1, i)
                        elif label == "last":
                            take_bank(pool, TURNS - 1, 1, "qk", 1, i)
                        elif not (isinstance(g, int) and g == 0):
                            take_bank(pool, t - 1, 1, "qk", 1, i)
                    tt(yr[:, 0:4], qr[:, 0:4], kr[:, 0:4], ALU.mult).then_inc(ym.sem, 1)
                elif part == 1:
                    tt(yr[:, 4:7], qr[:, 1:4], kr[:, 0:3], ALU.mult).then_inc(ym.sem, 1)
                elif part == 2:
                    tt(yr[:, 7], qr[:, 3], kr[:, 0], ALU.mult).then_inc(ym.sem, 1)
                else:
                    tt(yr[:, 8:10], qr[:, 2:4], kr[:, 0:2], ALU.mult).then_inc(ym.sem, 1)

            def products_aw(g, s, h, part):
                J2 = J // 2
                wr, ar, awr = leafwise(W[:, s], h), leafwise(A2[:], h), rows(AW[:])
                if part == 0:
                    wait(pool, a2, g, 1)
                    wait(pool, ws, g, 0)
                    wait(pool, om, g, 4 * h) if not (isinstance(g, int) and g == 0 and h == 0) else None
                    tt(awr[:, 0], RR[:, s, :, J2 * h:J2 * (h + 1)], wr[:, 0], ALU.mult).then_inc(awm.sem, 1)
                    tt(awr[:, 1:3], ar[:, 1:3], wr[:, 0:2], ALU.mult).then_inc(awm.sem, 1)
                else:
                    x = slice(HC2 * h, HC2 * (h + 1))
                    wait(pool, og, g, 1)
                    wait(pool, mg, g, 0)
                    tt(O[:, :, x], Q[:, s, :, x], F[:, s, :, x], ALU.mult).then_inc(om.sem, 1)

            def outputs(g, h, part):
                orr, yr, awr, x = leafwise(O[:], h), YV, rows(AW[:]), slice(HC2 * h, HC2 * (h + 1))
                i = 6 * h
                if part == 0:
                    wait(pool, yv, g, 4 * h + 4)
                wait(pool, om, g, i + 1 + part)
                if part == 0:
                    tt(orr[:, 1:4], orr[:, 1:4], yr[:, 4:7], ALU.add).then_inc(om.sem, 1)
                elif part == 1:
                    tt(orr[:, 3], orr[:, 3], awr[:, 0], ALU.add).then_inc(om.sem, 1)
                elif part == 2:
                    tt(orr[:, 2:4], orr[:, 2:4], awr[:, 1:3], ALU.add).then_inc(om.sem, 1)
                elif part == 3:
                    tt(O[:, :, x], O[:, :, x], A2[:, :, x], ALU.mult).then_inc(om.sem, 1)
                else:
                    tt(orr[:, 0:4], orr[:, 0:4], yr[:, 0:4], ALU.add).then_inc(om.sem, 1)

            def gate(t, g, s):
                wait(pool, aff, g, 1)
                if not (isinstance(t, int) and t == 0):
                    loaded(pool, "G", t - 1, s)
                    if s == 0:
                        wait(pool, am, t, 0)
                tt(OG[:, :, C * s:C * (s + 1)], O[:], G[:, s], ALU.mult).then_inc(og.sem, 1)

            def scale_right(t, s, j, which):
                g = t * 2 + s
                p, n, r0 = merge_of(j)
                b = (r0 - n) // R
                if which == 0:
                    wait(pool, gb, 2 * g + b // 8, 3)
                    wait(pool, mg, g, 2 * b) if b else wait(pool, cont, g, 4)
                elif b == 0:
                    wait(pool, cont, g, 8)
                gl = Gs[p][:, :, b >> p:(b >> p) + 1].to_broadcast([128, H, n])
                dst = Q[:, s, :, r0:r0 + n] if which else P[:, :, r0:r0 + n]
                tt(dst, dst, gl, ALU.mult).then_inc(psc.sem, 1)

            def scale_left(t, s, j):
                g = t * 2 + s
                p, n, r0 = merge_of(j)
                wait(pool, gb, 2 * g + r0 // R // 8, 3)
                wait(pool, tps, g, j + 1)
                wait(pool, wsc, g, pair_number(j))
                gr = Gs[p][:, :, (r0 // R) >> p].unsqueeze(1).unsqueeze(3).to_broadcast([128, n // R, H, R])
                dst = WT[:, (r0 - n) // R:r0 // R]
                tt(dst, dst, gr, ALU.mult).then_inc(wsc.sem, 1)

            def chunk(t, s):
                g, o = t * 2 + s, (s + 1) % 2
                here, nxt = 2 * s + 1, 2 * s + 2
                right = lambda j, *which: [scale_right(t, s, j, w) for w in which]
                kk = lambda c4, *parts: [products_kk(t, c4, x) for x in parts]
                qk = lambda h, *parts: [products_qk(t, g, s, o, h, x) for x in parts]
                aw = lambda h, *parts: [products_aw(g, o, h, x) for x in parts]
                out = lambda h, *parts: [outputs(g, h, x) for x in parts]
                kk(here, 0)
                right(1, 0)
                kk(here, 1)
                right(1, 1)
                kk(here, 2)
                scale_left(t, s, 1)
                right(3, 0, 1)
                kk(here, 3)
                leaf_diagonals(t, here)
                scale_left(t, s, 3)
                block_decays(t, here)
                qk(0, 0)
                right(5, 0, 1)
                qk(0, 1, 2, 3)
                scale_left(t, s, 5)
                aw(0, 0)
                right(7, 0, 1)
                scale_left(t, s, 7)
                qk(1, 0)
                right(9, 0, 1)
                qk(1, 1, 2, 3)
                scale_left(t, s, 9)
                right(11, 0, 1)
                gate(t, g, s)
                aw(0, 1)
                scale_left(t, s, 11)
                kk(nxt, 0, 1)
                right(13, 0, 1)
                kk(nxt, 2, 3)
                out(0, 0)
                scale_left(t, s, 13)
                out(0, 1, 2)
                aw(1, 0)
                out(0, 3, 4)
                leaf_diagonals(t, nxt)
                aw(1, 1)
                block_decays(t, nxt)
                out(1, 0, 1, 2, 3, 4)

            def last_outputs(g):
                gate(TURNS, g, 0)
                for h in range(2):
                    for part in range(4):
                        products_qk(TURNS, g, "last", 1, h, part)
                    if h == 0:
                        products_aw(g, 1, 0, 0)
                        products_aw(g, 1, 0, 1)
                for part in range(5):
                    outputs(g, 0, part)
                products_aw(g, 1, 1, 0)
                products_aw(g, 1, 1, 1)
                for part in range(5):
                    outputs(g, 1, part)
                gate(TURNS, g + 1, 1)

            for part in range(4):
                products_kk(0, 0, part)
            leaf_diagonals(0, 0)
            block_decays(0, 0)
            chunk(0, 0)
            chunk(0, 1)
            with pool.Fori(1, TURNS) as t:
                chunk(t, 0)
                chunk(t, 1)
            last_outputs(NCH)

        @block.vector
        def _(dve):
            tt = nc.vector.tensor_tensor
            for ap_ in (NC[:], KQ[:, 1], G[:], O[:], OG[:], ST[:], Q[:, 1]):
                nc.vector.memset(ap_, 0.0).then_inc(zeros.sem, 1)
            for c in (ws, mg, stu, wsc0):
                c.start(dve)
            dve.wait_ge(const.sem, 32)
            wait(dve, zeros, 0, 7)

            def decays(t, c4):
                s, h, g = c4 // 2 % 2, c4 % 2, t * 2 + c4 // 2
                i = t * 4 + c4
                loaded(dve, "A", t, c4 // 2)
                wait(dve, dcp, i, 2)
                if not (isinstance(t, int) and t == 0 and c4 < 2):
                    wait(dve, wt, g - 1, 8 * h + 8)
                    wait(dve, awm, g - 1, 2 * h + 1)
                    wait(dve, gb, i - 2, 1)
                    wait(dve, psc0, g - 1, 16 if h else 8)
                    wait(dve, wsc0, g - 1, 8 if h else 4)
                ar, fr, br = leafwise(A[:, s], h), leafwise(F[:, s], h), leafwise(B[:], h)
                J2 = J // 2
                rr = RR[:, s, :, J2 * h:J2 * (h + 1)]
                g0 = Gs[0][:, :, J2 * h:J2 * (h + 1)]
                tt(rr, ar[:, 1], ar[:, 2], ALU.mult).then_inc(dec.sem, 1)
                tt(fr[:, 2], ar[:, 0], ar[:, 1], ALU.mult).then_inc(dec.sem, 1)
                tt(br[:, 1], ar[:, 2], ar[:, 3], ALU.mult).then_inc(dec.sem, 1)
                wait(dve, dec, i, 1)
                tt(br[:, 0], rr, ar[:, 3], ALU.mult).then_inc(dec.sem, 1)
                wait(dve, dec, i, 2)
                tt(fr[:, 3], fr[:, 2], ar[:, 2], ALU.mult).then_inc(dec.sem, 1)
                wait(dve, dec, i, 5)
                tt(g0, fr[:, 3], ar[:, 3], ALU.mult).then_inc(dec.sem, 1)

            def row_pairs(t, c4, label):
                s, h, i = c4 // 2 % 2, c4 % 2, t * 4 + c4
                J2 = J // 2
                xr, ar = rows(X[:]), leafwise(A[:, s], h)
                wait(dve, dec, i, 1)
                loaded(dve, "A", t, c4 // 2)
                ps = take_bank(dve, t, label, "kk", h, 1)
                pr = ps[:, 0:3 * HJ2].rearrange("p (n h j) -> p n h j", n=3, h=H)
                tt(xr[:, 3], pr[:, 0], RR[:, s, :, J2 * h:J2 * (h + 1)], ALU.mult).then_inc(nl.sem, 1)
                tt(xr[:, 4:6], pr[:, 1:3], ar[:, 1:3], ALU.mult).then_inc(nl.sem, 1)

            def leaf_solution(t, c4, part):
                s, h, i = c4 // 2 % 2, c4 % 2, t * 4 + c4
                g = t * 2 + c4 // 2
                xr, n = rows(X[:]), NC[:, h]

                def row(t_, a, b):
                    return n[:, :, :, 5 * t_ + a:5 * t_ + b]

                def coef(k, cols):
                    return xr[:, k].unsqueeze(3).to_broadcast([128, H, J // 2, cols])

                def step(k, need, out, in0, in1, op):
                    if need > 2:
                        wait(dve, ncs, i, need - 2)
                    tt(out, in0, in1, op).then_inc(ncs.sem, 1)

                if part == 1:
                    wait(dve, nc0, i, 2)
                    wait(dve, nlc, i, 1)
                    wait(dve, nl, i, 2)
                    step(3, 1, row(1, 1, 2), coef(0, 1), row(0, 1, 2), ALU.mult)
                    step(4, 2, TMP[:, :, :, 0:1], coef(0, 1), row(0, 0, 1), ALU.mult)
                    step(5, 4, row(1, 0, 1), row(1, 0, 1), TMP[:, :, :, 0:1], ALU.add)
                    step(6, 0, TMP[:, :, :, 1:3], coef(4, 2), row(0, 0, 2), ALU.mult)
                    step(7, 0, row(2, 1, 3), coef(1, 2), row(1, 1, 3), ALU.mult)
                elif part == 2:
                    step(8, 7, TMP[:, :, :, 0:1], coef(1, 1), row(1, 0, 1), ALU.mult)
                    step(9, 8, row(2, 0, 1), row(2, 0, 1), TMP[:, :, :, 0:1], ALU.add)
                    step(10, 9, row(2, 0, 2), row(2, 0, 2), TMP[:, :, :, 1:3], ALU.add)
                    step(11, 10, row(3, 1, 4), coef(2, 3), row(2, 1, 4), ALU.mult)
                    step(12, 0, TMP[:, :, :, 0:1], coef(2, 1), row(2, 0, 1), ALU.mult)
                else:
                    step(13, 12, row(3, 0, 1), row(3, 0, 1), TMP[:, :, :, 0:1], ALU.add)
                    step(14, 0, TMP[:, :, :, 3:6], coef(5, 3), row(1, 0, 3), ALU.mult)
                    step(15, 14, row(3, 0, 3), row(3, 0, 3), TMP[:, :, :, 3:6], ALU.add)
                    step(16, 0, TMP[:, :, :, 1:3], coef(3, 2), row(0, 0, 2), ALU.mult)
                    step(17, 16, row(3, 0, 2), row(3, 0, 2), TMP[:, :, :, 1:3], ALU.add)

            def mask_gram(t, label, i):
                ps = take_bank(dve, t, label, "gram", i)
                p = {0: 0, 5: 0, 1: 1, 6: 1, 2: 2, 7: 2}[i]
                if p == 0:
                    n, m = 8, masks[0:64, 0, 0:64]
                    rs = 64
                else:
                    n, m, rs = 4, masks[:, p, :], 128
                v = lambda ap: ap.rearrange("p (n c) -> p n c", n=n)
                tt(v(BD[0:rs, i, :]), v(ps[0:rs, :]), m.unsqueeze(1).to_broadcast([rs, n, 512 // n]), ALU.mult)\
                    .then_inc(bd.sem, 1)

            def terms_qk(t, g, label, s, h):
                wr, yr, awr = leafwise(W[:, s], h), YV, rows(AW[:])
                v = lambda ps, n: ps[:, 0:n * HJ2].rearrange("p (n h j) -> p n h j", n=n, h=H)
                wait(dve, ws, g, 0)
                wait(dve, awm, g, 2 * h + 2)
                if h:
                    wait(dve, om, g, 6)
                else:
                    take_bank(dve, t, label, "var", 0)
                ps = take_bank(dve, t, label, "qk", h, 0)
                tt(yr[:, 0:4], v(ps, 4), wr[:, 0:4], ALU.mult).then_inc(yv.sem, 1)
                ps = take_bank(dve, t, label, "qk", h, 1)
                tt(yr[:, 4:7], v(ps, 4)[:, 0:3], wr[:, 0:3], ALU.mult).then_inc(yv.sem, 1)
                tt(awr[:, 0], v(ps, 4)[:, 3], awr[:, 0], ALU.mult).then_inc(yv.sem, 1)
                ps = take_bank(dve, t, label, "qk", h, 2)
                tt(awr[:, 1:3], v(ps, 2), awr[:, 1:3], ALU.mult).then_inc(yv.sem, 1)

            def center(t, g, label):
                for i in range(2):
                    ps = take_bank(dve, t, label, "mean", i)
                    o = O[:, 8 * i:8 * (i + 1), :]
                    tt(o, o, ps[:].rearrange("p (h c) -> p h c", h=8), ALU.subtract).then_inc(oc.sem, 1)

            def invert(g):
                wait(dve, sd, g, 1)
                nc.vector.reciprocal(rdev[:], sdev[:]).then_inc(rd.sem, 1)

            def norm(t, g, label, halves=(0, 1)):
                for i in halves:
                    ps = take_bank(dve, t, label, "rstd", i)
                    o = O[:, 8 * i:8 * (i + 1), :]
                    tt(o, o, ps[:].rearrange("p (h c) -> p h c", h=8), ALU.mult).then_inc(on.sem, 1)

            def decay_state(t, g, s, i):
                wait(dve, cont, g, 8)
                ps = take_bank(dve, t, s, "decay", i)
                x = ST[:, 4 * i:4 * i + 4, :]
                tt(x, x, ps[:].rearrange("p (h v) -> p h v", h=4), ALU.mult).then_inc(stg.sem, 1)

            def scale_leaf(g, s, j, which):
                gl = Gs[0][:, :, j:j + 1].to_broadcast([128, H, R])
                r0 = R * (j + 1)
                wait(dve, mg, g, 2 * j - 1 + which) if j else wait(dve, cont, g, 4 + 4 * which)
                dst = Q[:, s, :, r0:r0 + R] if which else P[:, :, r0:r0 + R]
                tt(dst, dst, gl, ALU.mult).then_inc(psc0.sem, 1)

            def scale_leaf_w(g, s, j):
                if j % 2:
                    return
                wait(dve, tps, g, j + 1)
                tt(WT[:, j], WT[:, j], Gs[0][:, :, j + 1:j + 2].to_broadcast([128, H, R]), ALU.mult).then_inc(wsc0.sem, 1)

            def add_merged(g, s, j, which):
                p, n, r0 = merge_of(j)
                m = psM[:, 512 * which:512 * which + H * n].rearrange("p (h t) -> p h t", h=H)
                wait(dve, mps, g, 2 * j + 1 + which)
                wait(dve, psc if p else psc0, g, 2 * pair_number(j) + 1 + which)
                x = Q[:, s, :, r0:r0 + n] if which else P[:, :, r0:r0 + n]
                tt(x, x, m, ALU.add).then_inc(mg.sem, 1)

            def chunk(t, s):
                g, o = t * 2 + s, (s + 1) % 2
                here, nxt = 2 * s + 1, 2 * s + 2
                for j in range(J):
                    jj, h = j % 8, j // 8
                    if j == 0 or j == 8:
                        wait(dve, ncs, 2 * g + h, NCS)
                    lf = slice(R * j, R * (j + 1))
                    eq = NC[:, h, :, jj, :].rearrange("p h (t c) -> p h t c", c=R + 1)
                    if j == 0:
                        wait(dve, cont, g, 4)
                        if not (isinstance(t, int) and t == 0 and s == 0):
                            wait(dve, yv, g, 0)
                    else:
                        wait(dve, mg, g, 2 * j - 1)
                    tt(eq[:, :, :, 1:5], eq[:, :, :, 1:5], P[:, :, lf].unsqueeze(2).to_broadcast([128, H, R, R]), ALU.mult)\
                        .then_inc(ap.sem, 1)
                    wait(dve, ap, g, j + 1)
                    nc.vector.tensor_reduce(W[:, s, :, lf], eq, AXIS.X, ALU.add).then_inc(ws.sem, 1)
                    wait(dve, ws, g, j + 1)
                    tt(WT[:, j], W[:, s, :, lf], B[:, :, lf], ALU.mult).then_inc(wt.sem, 1)

                    if j:
                        if j == 1:
                            scale_leaf(g, s, 0, 1)
                        add_merged(g, s, j - 1, 1)
                    if j % 2 == 0:
                        scale_leaf(g, s, j, 0)
                        if j:
                            scale_leaf(g, s, j, 1)
                    if j == 1:
                        decays(t, here)
                    elif j == 2:
                        center(t, g, s)
                    elif j == 3:
                        mask_gram(t, s, 2)
                    elif j == 4:
                        row_pairs(t, here, s)
                        leaf_solution(t, here, 1)
                    elif j == 5:
                        leaf_solution(t, here, 2)
                    elif j == 6:
                        invert(g)
                    elif j == 7:
                        terms_qk(t, g, s, o, 0)
                        leaf_solution(t, here, 3)
                    elif j == 8:
                        mask_gram(t, s, 5)
                        norm(t, g, s, (0,))
                    elif j == 9:
                        mask_gram(t, s, 6)
                        norm(t, g, s, (1,))
                        decay_state(t, g, s, 0)
                    elif j == 10:
                        decay_state(t, g, s, 1)
                        decay_state(t, g, s, 2)
                    elif j == 11:
                        mask_gram(t, s, 7)
                        decays(t, nxt)
                    elif j == 12:
                        decay_state(t, g, s, 3)
                    elif j == 14:
                        row_pairs(t, nxt, s)
                        mask_gram(t, s, 0)
                    elif j == 15:
                        terms_qk(t, g, s, o, 1)
                        leaf_solution(t, nxt, 1)
                        mask_gram(t, s, 1)

                    if j < JM:
                        scale_leaf_w(g, s, j)
                        add_merged(g, s, j, 0)
                wait(dve, stg, g, 4)
                for i in range(4):
                    ps = take_bank(dve, t, s, "update", i)
                    x = ST[:, i % 2 + 8 * (i // 2):8 * (i // 2) + 8:2, :]
                    tt(x, x, ps[:].rearrange("p (h v) -> p h v", h=4), ALU.add).then_inc(stu.sem, 1)
                leaf_solution(t, nxt, 2)
                leaf_solution(t, nxt, 3)

            decays(0, 0)
            row_pairs(0, 0, "first")
            for part in (1, 2, 3):
                leaf_solution(0, 0, part)
            for i in range(2):
                mask_gram(0, "first", i)
            chunk(0, 0)
            chunk(0, 1)
            with dve.Fori(1, TURNS) as t:
                chunk(t, 0)
                chunk(t, 1)
            center(TURNS, NCH, "last")
            invert(NCH)
            norm(TURNS, NCH, "last")
            for h in range(2):
                terms_qk(TURNS, NCH, "last", 1, h)
            center(TURNS, NCH + 1, "end")
            invert(NCH + 1)
            norm(TURNS, NCH + 1, "end")

        @block.scalar
        def _(act):
            copy = lambda out, in_: nc.scalar.activation(out, in_, ACT.Copy)
            for c in (ktok, wl):
                c.start(act)
            act.wait_ge(const.sem, 32)
            wait(act, zeros, 0, 7)
            act.wait_ge(cl.sem, cl.at(0, 2))

            def decay_copies(t, c4):
                s, h, g = c4 // 2 % 2, c4 % 2, t * 2 + c4 // 2
                loaded(act, "A", t, c4 // 2)
                if not (isinstance(t, int) and t == 0 and c4 < 2):
                    wait(act, ncs, t * 4 + c4 - 1, 0)
                    wait(act, wt, g - 1, 8 * h + 8)
                    wait(act, om, g - 1, 6 * h + 1)
                ar = leafwise(A[:, s], h)
                copy(leafwise(F[:, s], h)[:, 1], ar[:, 0]).then_inc(dcp.sem, 1)
                copy(leafwise(B[:], h)[:, 2], ar[:, 3]).then_inc(dcp.sem, 1)

            def k_compact(t, c4):
                s, h, g = c4 // 2 % 2, c4 % 2, t * 2 + c4 // 2
                loaded(act, "K", t, c4 // 2)
                if not (isinstance(t, int) and t == 0 and c4 == 0):
                    if h:
                        wait(act, bd, g, 3)
                    else:
                        wait(act, bd, g, 0)
                        wait(act, bda, g, 0)
                kx, c0 = KQ[:, s, 0], HC2 * h
                copy(KL[:], kx[:, :, c0:c0 + HC2].rearrange("p h (j r) -> p j h r", r=R)).then_inc(kc.sem, 1)
                copy(KC[:, 0].rearrange("p (h t) -> p h t", h=H), kx[:, :, c0:c0 + 16]).then_inc(kc.sem, 1)
                if h == 0:
                    copy(KC[:, 1:3].rearrange("p n (h t) -> p (n h) t", t=32), kx[:, :, 0:32]).then_inc(kc.sem, 1)

            def pairs_copy(t, c4, label):
                ps = take_bank(act, t, label, "kk", c4 % 2, 0)
                copy(X[:, 0:3, :].rearrange("p n c -> p (n c)"), ps[:, 0:3 * HJ2]).then_inc(nlc.sem, 1)

            def contact_copy(t, s, q):
                g = t * 2 + s
                if not (isinstance(t, int) and t == 0 and s == 0):
                    wait(act, mg, g, 0)
                    wait(act, om, g, 0) if q else wait(act, ws, g, 0)
                for i in range(4):
                    ps = take_bank(act, t, s, "contact", i)
                    dst = (P[:], Q[:, s])[q][:, 4 * i:4 * i + 4, :]
                    copy(dst, ps[:].rearrange("p (h q t) -> p q h t", h=4, q=2)[:, q]).then_inc(cont.sem, 1)

            def mask_gram_act(t, label, i):
                g = t * 2 + label
                ps = take_bank(act, t, label, "gram", i)
                v = lambda ap: ap.rearrange("p (n m c) -> p n m c", n=4, m=4)
                for m in range(4):
                    last = nc.scalar.activation(v(BD[:, i, :])[:, :, m], v(ps[:])[:, :, m], ACT.Copy,
                                                scale=masks[:, 3, 32 * m:32 * m + 1])
                last.then_inc(bda.sem, 1)

            def squares(t, g):
                wait(act, oc, g, 2)
                nc.scalar.activation(SQ[:], O[:], ACT.Square).then_inc(sqd.sem, 1)

            def deviation(t, g, label):
                ps = take_bank(act, t, label, "var", 0)
                if not (isinstance(g, int) and g == 0):
                    wait(act, rd, g, 0)
                nc.scalar.activation(sdev[:], ps[:, 0:8], ACT.Sqrt, bias=eps[:, 0:1]).then_inc(sd.sem, 1)

            def affine(g):
                wait(act, on, g, 2)
                nc.scalar.activation(O[:], O[:], ACT.Identity, scale=lng[:, 0:1], bias=lnb[:, 0:1]).then_inc(aff.sem, 1)

            def att_copy(t, label):
                ps = take_bank(act, t, label, "wo", 0)
                if not (isinstance(t, int) and t == 0):
                    wait(act, ast, t, 0)
                copy(att[:], ps[:, 0:HID]).then_inc(am.sem, 1)

            w_end = lambda a, b: WE[:, :, R * a:R * b].rearrange("p h (l r) -> p h l r", r=R)
            w_leaves = lambda a, b: WT[:, a:b].rearrange("p l h r -> p h l r")

            def chunk(t, s):
                g, o = t * 2 + s, (s + 1) % 2
                first = isinstance(t, int) and t == 0 and s == 0
                contact_copy(t, s, 0)
                contact_copy(t, s, 1)
                for j in range(J):
                    if j < JM:
                        p, n, r0 = merge_of(j)
                        if p >= 2:
                            wait(act, wt, g, j + 1)
                            wait(act, wsc, g, pair_number(j))
                            wait(act, wsc0, g, pair_number(j) + 1)
                            wait(act, tps, g, j)
                            copy(WC[:, 0:H * n].rearrange("p (h l r) -> p h l r", h=H, r=R),
                                 WT[:, (r0 - n) // R:r0 // R].rearrange("p l h r -> p h l r")).then_inc(wc.sem, 1)
                        wait(act, tps, g, j + 1)
                        wait(act, mps, g, 2 * j)
                        w_ = 128 << max(p - 1, 0)
                        copy(WL[:, 0:w_], psT[:, 0:w_]).then_inc(wl.sem, 1)
                    if j == 13:
                        wait(act, wsc, g, 6)
                        wait(act, wsc0, g, 6)
                        copy(w_end(0, 12), w_leaves(0, 12)).then_inc(wec.sem, 1)
                    if j == 0:
                        decay_copies(t, 2 * s + 1)
                    elif j == 2:
                        if not first:
                            loaded(act, "A", t, s - 1)
                            wait(act, om, g, 0)
                        copy(A2[:], A[:, o]).then_inc(a2.sem, 1)
                    elif j == 3:
                        pairs_copy(t, 2 * s + 1, s)
                        squares(t, g)
                    elif j == 4:
                        k_compact(t, 2 * s + 1)
                        mask_gram_act(t, s, 3)
                    elif j == 5:
                        deviation(t, g, s)
                        mask_gram_act(t, s, 4)
                    elif j == 9:
                        affine(g)
                    elif j == 10:
                        decay_copies(t, 2 * s + 2)
                    elif j == 11:
                        if s == 1:
                            att_copy(t, s)
                    elif j == 12:
                        k_compact(t, 2 * s + 2)
                        for i in range(2):
                            ps = take_bank(act, t, s, "ktok", i)
                            wait(act, stu, g, 0)
                            copy(KTOK[:, 4 * i:4 * i + 4, :].rearrange("p n c -> p (n c)"), ps[:]).then_inc(ktok.sem, 1)
                    elif j == 13:
                        pairs_copy(t, 2 * s + 2, s)
                wait(act, wt, g, J)
                wait(act, wsc, g, JM // 2)
                wait(act, wsc0, g, JM // 2 + 1)
                copy(w_end(12, J), w_leaves(12, J)).then_inc(wec.sem, 1)
                for i in range(2):
                    ps = take_bank(act, t, s, "wtok", i)
                    wait(act, stu, g, 0)
                    copy(WTOK[:, 4 * i:4 * i + 4, :].rearrange("p n c -> p (n c)"), ps[:]).then_inc(wtok.sem, 1)

            decay_copies(0, 0)
            k_compact(0, 0)
            pairs_copy(0, 0, "first")
            chunk(0, 0)
            chunk(0, 1)
            with act.Fori(1, TURNS) as t:
                chunk(t, 0)
                chunk(t, 1)
            loaded(act, "A", TURNS, -1)
            wait(act, om, NCH, 0)
            copy(A2[:], A[:, 1]).then_inc(a2.sem, 1)
            for i, label in enumerate(("last", "end")):
                squares(TURNS, NCH + i)
                deviation(TURNS, NCH + i, label)
                affine(NCH + i)
            att_copy(TURNS, "end")

        @block.tensor
        def _(pe):
            mm = nc.tensor.matmul
            for c in (mps,):
                c.start(pe)
            pe.wait_ge(const.sem, 32)
            wait(pe, zeros, 0, 7)

            def shared_job(t, label, job):
                kind, n = job[0], job[-1]
                g = {"first": 0, "last": NCH, "end": NCH + 1}[label] if isinstance(label, str) else t * 2 + label
                s = {"first": 0, "last": 1, "end": 1}.get(label, label)
                ps, filled = open_bank(pe, t, label, *job)
                if kind == "contact":
                    wait(pe, stu, g, -2 if n < 2 else 0)
                    if n == 0:
                        loaded(pe, "K", t, s)
                        loaded(pe, "Q", t, s)
                    for m in range(4):
                        h = 4 * n + m
                        last = mm(ps[:, 128 * m:128 * (m + 1)], ST[:, h, :], KQ[:, s, :, h, :], start=True, stop=True)
                elif kind == "kk":
                    i = 0 if label == "first" else g * 2 + (1 if job[1] else 2)
                    wait(pe, xm, i, 3 if n else 1)
                    last = mm(ps[:, 0:3 * HJ2], ones[:], X[:, 3 * n:3 * n + 3, :].rearrange("p n c -> p (n c)"),
                              start=True, stop=True)
                elif kind == "gram":
                    gs, gi = (s, g) if (n >= 2 or label == "first") else ((s + 1) % 2, g + 1)
                    ci = 0 if label == "first" else label + (n < 2)
                    loaded(pe, "K", t, ci)
                    loaded(pe, "Q", t, ci)
                    wait(pe, kc, gi, 3 if n < 5 else 5)
                    for (j, i), (bank, col) in grams.items():
                        if bank != n:
                            continue
                        p, w_, r0 = merge_of(j)
                        hp = H if p == 0 else 128 // w_
                        hs = slice(i * hp, (i + 1) * hp)
                        rs = hp * w_
                        l0 = (r0 - w_) % HC2 // R
                        if p < 2:
                            left = KL[:, l0:l0 + w_ // R].rearrange("p l h r -> p (l h r)")
                        else:
                            left = KC[:].rearrange("p n c -> p (n c)")[:, (256 if p == 3 else 0) + rs * i:][:, 0:rs]
                        last = mm(ps[0:rs, col:col + 2 * rs], left, KQ[:, gs, :, hs, r0:r0 + w_],
                                  start=True, stop=True)
                elif kind == "ktok":
                    for m in range(4):
                        i = 4 * n + m
                        last = nc.tensor.transpose(ps[:, 128 * m:128 * (m + 1)], KQ[:, s, 0, 2 * i:2 * i + 2, :].rearrange("p h c -> p (h c)"), ident[:])
                elif kind == "decay":
                    wait(pe, g4, g, 1)
                    for m in range(4):
                        last = nc.tensor.transpose(ps[:, 128 * m:128 * (m + 1)],
                                                   Gs[4][:, 4 * n + m, :].to_broadcast([128, 128]), ident[:])
                elif kind == "qk":
                    h = job[1]
                    wait(pe, ym, g, 4 * h + (1, 3, 4)[n])
                    a, b = ((0, 4), (4, 8), (8, 10))[n]
                    last = mm(ps[:, 0:(b - a) * HJ2], ones[:], Y[:, a:b, :].rearrange("p n c -> p (n c)"), start=True, stop=True)
                elif kind == "mean":
                    if not (isinstance(g, int) and g == 0):
                        wait(pe, om, g, 0)
                    last = mm(ps[:], avg[:], O[:, 8 * n:8 * n + 8, :].rearrange("p h c -> p (h c)"), start=True, stop=True)
                elif kind == "var":
                    wait(pe, sqd, g, 1)
                    for i in range(8):
                        last = mm(ps[:, i:i + 1], SQ[:, 2 * i:2 * i + 2, :].rearrange("p h c -> p (h c)"), avg[:, 0:1],
                                  start=True, stop=True)
                elif kind == "rstd":
                    wait(pe, rd, g, 1)
                    for m in range(4):
                        i = 4 * n + m
                        last = nc.tensor.transpose(ps[:, 128 * m:128 * (m + 1)],
                                                   rdev[:, i:i + 1].to_broadcast([128, 128]), ident[:])
                elif kind == "wo":
                    wait(pe, wol, 0, 1)
                    wait(pe, og, g, 1)
                    for h in range(H):
                        last = mm(ps[:, 0:HID], OG[:, h, :], wo[:, h, :], start=h == 0, stop=h == H - 1)
                elif kind == "wtok":
                    wait(pe, wec, g, 2)
                    for m in range(4):
                        i = 4 * n + m
                        last = nc.tensor.transpose(ps[:, 128 * m:128 * (m + 1)],
                                                   WE[:, 2 * i:2 * i + 2, :].rearrange("p h c -> p (h c)"), ident[:])
                elif kind == "update":
                    wait(pe, wtok, g, n // 2 + 1)
                    wait(pe, ktok, g, 2)
                    r = slice(64 * (n % 2), 64 * (n % 2) + 64)
                    for m in range(4):
                        i = 4 * (n // 2) + m
                        last = mm(ps[:, 128 * m:128 * (m + 1)], KTOK[r, i, :], WTOK[r, i, :], start=True, stop=True)
                last.then_inc(filled, 1)

            def chunk(t, s):
                g = t * 2 + s
                for i in range(4):
                    shared_job(t, s, ("contact", i))
                for j in range(J):
                    if j < JM:
                        p, n, r0 = merge_of(j)
                        tiles, hp = (1, H) if p == 0 else (1 << (p - 1), 128 // n)
                        rs = hp * n
                        wait(pe, wt, g, j + 1)
                        if p == 1:
                            wait(pe, wsc0, g, pair_number(j) + 1)
                        elif p >= 2:
                            wait(pe, wc, g, {3: 1, 7: 2, 11: 3}[j])
                        wait(pe, wl, g, j)
                        for i in range(tiles):
                            left = (WT[:, j - p:j - p + 2].rearrange("p l h r -> p (l h r)") if p < 2
                                    else WC[:, 128 * i:128 * (i + 1)])
                            last = nc.tensor.transpose(psT[:, 128 * i:128 * (i + 1)], left, ident[:])
                        last.then_inc(tps.sem, 1)
                        ready, k = masked(max(grams[j, i][0] for i in range(tiles)))
                        wait(pe, ready, g, k)
                        wait(pe, wl, g, j + 1)
                        for q in range(2):
                            wait(pe, mg, g, 2 * j - 1 + q)
                            for i in range(tiles):
                                bank, col = grams[j, i]
                                last = mm(psM[:, 512 * q + rs * i:512 * q + rs * (i + 1)], WL[0:rs, 128 * i:128 * (i + 1)],
                                          BD[0:rs, bank, col + rs * q:col + rs * (q + 1)], start=True, stop=True)
                            last.then_inc(mps.sem, 1)
                    for job in leaf_jobs(s, j):
                        shared_job(t, s, job)
                for i in range(2):
                    shared_job(t, s, ("wtok", i))
                shared_job(t, s, ("gram", 1))
                for i in range(4):
                    shared_job(t, s, ("update", i))

            for job in PROLOGUE:
                shared_job(0, "first", job[1:])
            chunk(0, 0)
            chunk(0, 1)
            with pe.Fori(1, TURNS) as t:
                chunk(t, 0)
                chunk(t, 1)
            for job in EPILOGUE:
                shared_job(TURNS, job[0], job[1:])


def feed_forward(nc, ident, x_d, att_d, gate_d, gbias_d, wg_d, wu_d, wd_d, out_d):
    ctx = ExitStack()
    with ctx:
        sb = lambda name, shape: ctx.enter_context(nc.sbuf_tensor("C_" + name, shape, FP32))
        sem = lambda name: ctx.enter_context(nc.semaphore("C_" + name))
        NT = TF // 128
        wg, wu = sb("wg", [128, KT, HROWS]), sb("wu", [128, KT, HROWS])
        wd = sb("wd", [128, MT, HID])
        gate, gbias = sb("gate", [128, KT, E]), sb("gbias", [128, E])
        eps = sb("eps", [128, 1])
        spread = sb("spread", [E, E * HE])
        rank = sb("rank", [128, NT, E])
        x, at = sb("x", [128, 2, NT, HID]), sb("at", [128, 2, NT, HID])
        x1, xc, xn = sb("x1", [128, NT, HID]), sb("xc", [128, NT, HID]), sb("xn", [128, NT, HID])
        stat, std = sb("stat", [128, 3 * NT]), sb("std", [128, 2 * NT])
        xT = sb("xT", [128, KT, TF])
        score = sb("score", [128, NT, E])
        key, pick, tmp, wsel = [sb(n, [128, NT, E]) for n in ("key", "pick", "tmp", "wsel")]
        best, inv = sb("best", [128, NT]), sb("inv", [128, NT])
        wT = sb("wT", [E, TF])
        act_g = sb("act_g", [128, 2, TF])
        hid = sb("hid", [128, MT, TF])
        y = sb("y", [128, NT, HID])
        psG = [ctx.enter_context(nc.psum_tensor(f"C_psG{i}", [128, 512], FP32)) for i in range(2)]
        psU = [ctx.enter_context(nc.psum_tensor(f"C_psU{i}", [128, 512], FP32)) for i in range(2)]
        psW = [ctx.enter_context(nc.psum_tensor(f"C_psW{i}", [128, 512], FP32)) for i in range(2)]
        psX = [ctx.enter_context(nc.psum_tensor(f"C_psX{i}", [128, 512], FP32)) for i in range(2)]
        gate_ld, hidden_ld, down_ld, const = sem("gate_ld"), sem("hidden_ld"), sem("down_ld"), sem("const")
        x_ld = [Count(sem(f"x_ld{s}"), 2, 16) for s in range(2)]
        ROUTE = 19
        x1m, ln, var = Count(sem("x1_made"), 1), Count(sem("ln"), 6), Count(sem("var"), 1)
        sd, xnm = Count(sem("std"), 1), Count(sem("xn_made"), 1)
        xtp, xtm = Count(sem("xT_ps"), 2), Count(sem("xT_made"), 2)
        gp, sc = Count(sem("gate_ps"), 1), Count(sem("score"), 1)
        rt = Count(sem("routing"), ROUTE)
        wp, wm = Count(sem("weights_ps"), 1), Count(sem("weights_made"), 1)
        gu, gs = Count(sem("hidden_ps"), MT), Count(sem("silu"), MT)
        wb = Count(sem("spread_ps"), ET)
        hm, hw = Count(sem("hidden"), MT, 1, 1), Count(sem("hidden_weighted"), ET, 1, 1)
        dn, ym = Count(sem("down_ps"), NT), Count(sem("y_made"), NT, 1, 1)
        st = Count(sem("out_st"), 1, 16, 1)
        order = list(range(ET, MT)) + list(range(ET))

        def wait(eng, c, index, k):
            eng.wait_ge(c.sem, c.at(index, k))

        block = ctx.enter_context(nc.Block())

        @block.sync
        def _(sp):
            st.start(sp)

            def load(t, s, at0):
                for dst, src in ((x, x_d), (at, att_d)):
                    sp.dma_start(dst[:, s], src[bass.ds(at0, TF), :].rearrange("(n p) c -> p n c", p=128))\
                      .then_inc(x_ld[s].sem, 16)

            load(0, 0, 0)
            sp.dma_start(gate[:], gate_d.rearrange("(k p) e -> p k e", p=128)).then_inc(gate_ld, 16)
            sp.dma_start(gbias[:], gbias_d.partition_broadcast(128)).then_inc(gate_ld, 16)
            sp.dma_start(wg[:], wg_d.rearrange("(k p) n -> p k n", p=128)).then_inc(hidden_ld, 16)
            sp.dma_start(wu[:], wu_d.rearrange("(k p) n -> p k n", p=128)).then_inc(hidden_ld, 16)
            sp.dma_start(wd[:, 0:MT - 1, :], wd_d[0:128 * (MT - 1), :].rearrange("(m p) c -> p m c", p=128)).then_inc(down_ld, 16)
            sp.dma_start(wd[0:MROWS[-1], MT - 1, :], wd_d[128 * (MT - 1):HROWS, :]).then_inc(down_ld, 16)
            load(0, 1, TF)
            with sp.Fori(0, NTF // 2) as t:
                for s in range(2):
                    i = t * 2 + s
                    wait(sp, ym, i, NT)
                    sp.dma_start(out_d[bass.ds(t * (2 * TF) + s * TF, TF), :].rearrange("(n p) c -> p n c", p=128), y[:])\
                      .then_inc(st.sem, 16)
                    sp.wait_ge(x1m.sem, x1m.at(i, 1))
                    for dst, src in ((x, x_d), (at, att_d)):
                        sp.dma_start(dst[:, s], src[bass.ds(((t + 1) % (NTF // 2)) * (2 * TF) + s * TF, TF), :]
                                     .rearrange("(n p) c -> p n c", p=128)).then_inc(x_ld[s].sem, 16)
            wait(sp, st, NTF, 0)
            for s in range(2):
                wait(sp, x_ld[s], NTF // 2, 2)

        @block.gpsimd
        def _(pool):
            n = 0
            for m, v in ((eps[:], EPS), (spread[:], 1.0)):
                nc.gpsimd.memset(m, v).then_inc(const, 1)
                n += 1
            for e in range(E):
                nc.gpsimd.memset(rank[:, :, e:e + 1], float(E - e)).then_inc(const, 1)
                n += 1
            for base_, step, sign in ((0, 1, -HE), (HE - 1, -1, HE)):
                pool.wait_ge(const, n)
                nc.gpsimd.affine_select(out=spread[:], in_=spread[:], compare_op=ALU.is_ge, fill=0.0, base=base_,
                                        pattern=[[step, E * HE]], channel_multiplier=sign).then_inc(const, 1)
                n += 1
            pool.wait_ge(const, n)

        NCONST = 2 + E + 2

        @block.vector
        def _(dve):
            tt = nc.vector.tensor_tensor
            for c in (hm, hw, ym):
                c.start(dve)
            dve.wait_ge(const, NCONST)
            dve.wait_ge(gate_ld, 32)

            def normalize(t, s):
                i = t * 2 + s
                wait(dve, x_ld[s], t, 2)
                if s == 0:
                    wait(dve, ym, i, 0)
                else:
                    wait(dve, ym, i, 0)
                tt(x1[:], x[:, s], at[:, s], ALU.add).then_inc(x1m.sem, 1)
                bc = lambda v: v.unsqueeze(2).to_broadcast([128, NT, HID])
                mean, ssq, va = stat[:, 0:NT], stat[:, NT:2 * NT], stat[:, 2 * NT:3 * NT]
                wait(dve, x1m, i, 1)
                nc.vector.tensor_reduce(ssq, x1[:], AXIS.X, ALU.add).then_inc(ln.sem, 1)
                wait(dve, ln, i, 1)
                nc.vector.tensor_scalar(mean, ssq, 1.0 / HID, None, ALU.mult).then_inc(ln.sem, 1)
                wait(dve, ln, i, 2)
                tt(xc[:], x1[:], bc(mean), ALU.subtract).then_inc(ln.sem, 1)
                wait(dve, ln, i, 3)
                tt(xn[:], xc[:], xc[:], ALU.mult).then_inc(ln.sem, 1)
                wait(dve, ln, i, 4)
                nc.vector.tensor_reduce(ssq, xn[:], AXIS.X, ALU.add).then_inc(ln.sem, 1)
                wait(dve, ln, i, 5)
                nc.vector.tensor_scalar(va, ssq, 1.0 / HID, None, ALU.mult).then_inc(var.sem, 1)
                wait(dve, sd, i, 1)
                nc.vector.reciprocal(std[:, NT:2 * NT], std[:, 0:NT]).then_inc(ln.sem, 1)
                wait(dve, ln, i, 6)
                tt(xn[:], xc[:], bc(std[:, NT:2 * NT]), ALU.mult).then_inc(xnm.sem, 1)

            def route(i):
                wait(dve, sc, i, 1)
                n = [0]

                def step(ins):
                    n[0] += 1
                    ins.then_inc(rt.sem, 1)
                    wait(dve, rt, i, n[0])

                bc = lambda v: v.unsqueeze(2).to_broadcast([128, NT, E])
                step(tt(key[:], score[:], gbias[:].unsqueeze(1).to_broadcast([128, NT, E]), ALU.add))
                for k in range(TOPK):
                    step(nc.vector.tensor_reduce(best[:], key[:], AXIS.X, ALU.max))
                    step(tt(tmp[:], key[:], bc(best[:]), ALU.is_equal))
                    step(tt(tmp[:], tmp[:], rank[:], ALU.mult))
                    step(nc.vector.tensor_reduce(best[:], tmp[:], AXIS.X, ALU.max))
                    step(tt(tmp[:], rank[:], bc(best[:]), ALU.is_equal))
                    if k == 0:
                        step(nc.vector.tensor_copy(pick[:], tmp[:]))
                        step(nc.vector.tensor_scalar(tmp[:], tmp[:], -1e30, None, ALU.mult))
                        step(tt(key[:], key[:], tmp[:], ALU.add))
                    else:
                        step(tt(pick[:], pick[:], tmp[:], ALU.add))
                step(tt(wsel[:], score[:], pick[:], ALU.mult))
                step(nc.vector.tensor_reduce(best[:], wsel[:], AXIS.X, ALU.add))
                step(nc.vector.reciprocal(inv[:], best[:]))
                step(tt(wsel[:], wsel[:], bc(inv[:]), ALU.mult))
                assert n[0] == rt.per

            def tile(t, s):
                i = t * 2 + s
                normalize(t, s)
                for k, m in enumerate(order):
                    r = MROWS[m]
                    wait(dve, gs, i, k + 1)
                    tt(hid[0:r, m, :], act_g[0:r, k % 2, :], psU[k % 2][0:r, :], ALU.mult).then_inc(hm.sem, 1)
                    if m < ET:
                        wait(dve, wb, i, m + 1)
                        wait(dve, hm, i, k + 1)
                        tt(hid[:, m, :], hid[:, m, :], psW[m % 2][:], ALU.mult).then_inc(hw.sem, 1)
                    if k == 0:
                        route(i)
                for n in range(NT):
                    wait(dve, dn, i, n + 1)
                    wait(dve, st, i, 0)
                    tt(y[:, n, :], x1[:, n, :], psX[n % 2][:, 0:HID], ALU.add).then_inc(ym.sem, 1)

            with dve.Fori(0, NTF // 2) as t:
                tile(t, 0)
                tile(t, 1)

        @block.scalar
        def _(act):
            act.wait_ge(const, NCONST)

            def tile(t, s):
                i = t * 2 + s
                wait(act, var, i, 1)
                nc.scalar.activation(std[:, 0:NT], stat[:, 2 * NT:3 * NT], ACT.Sqrt, bias=eps[:, 0:1]).then_inc(sd.sem, 1)
                for kt in range(KT):
                    wait(act, xtp, i, kt + 1)
                    nc.scalar.activation(xT[:, kt, :], psX[kt][:], ACT.Copy).then_inc(xtm.sem, 1)
                wait(act, gp, i, 1)
                nc.scalar.activation(score[:].rearrange("p n e -> p (n e)"), psX[0][:, 0:NT * E], ACT.Sigmoid)\
                    .then_inc(sc.sem, 1)
                for k, m in enumerate(order):
                    if k == 3:
                        wait(act, wp, i, 1)
                        nc.scalar.activation(wT[:], psX[1][0:E, :], ACT.Copy).then_inc(wm.sem, 1)
                    r = MROWS[m]
                    wait(act, gu, i, k + 1)
                    wait(act, hm, i, k - 1)
                    nc.scalar.activation(act_g[0:r, k % 2, :], psG[k % 2][0:r, :], ACT.Silu).then_inc(gs.sem, 1)

            with act.Fori(0, NTF // 2) as t:
                tile(t, 0)
                tile(t, 1)

        @block.tensor
        def _(pe):
            mm = nc.tensor.matmul
            pe.wait_ge(gate_ld, 32)
            pe.wait_ge(const, NCONST)

            def tile(t, s):
                i = t * 2 + s
                wait(pe, xnm, i, 1)
                wait(pe, ym, i, 0)
                for kt in range(KT):
                    for n in range(NT):
                        last = nc.tensor.transpose(psX[kt][:, 128 * n:128 * (n + 1)], xn[:, n, 128 * kt:128 * (kt + 1)], ident[:])
                    last.then_inc(xtp.sem, 1)
                wait(pe, xtm, i, 2)
                for n in range(NT):
                    for kt in range(KT):
                        last = mm(psX[0][:, E * n:E * (n + 1)], xT[:, kt, 128 * n:128 * (n + 1)], gate[:, kt, :],
                                  start=kt == 0, stop=kt == KT - 1)
                last.then_inc(gp.sem, 1)
                pe.wait_ge(hidden_ld, 32)
                for k, m in enumerate(order):
                    r = MROWS[m]
                    if k == 3:
                        wait(pe, rt, i, ROUTE)
                        for n in range(NT):
                            last = nc.tensor.transpose(psX[1][0:E, 128 * n:128 * (n + 1)], wsel[:, n, :], ident[:])
                        last.then_inc(wp.sem, 1)
                        wait(pe, wm, i, 1)
                    wait(pe, hm, i, k - 1)
                    for ps, w in ((psG, wg), (psU, wu)):
                        for kt in range(KT):
                            last = mm(ps[k % 2][0:r, :], w[:, kt, 128 * m:128 * m + r], xT[:, kt, :],
                                      start=kt == 0, stop=kt == KT - 1)
                    last.then_inc(gu.sem, 1)
                    if m < ET:
                        wait(pe, hw, i, m - 1)
                        mm(psW[m % 2][:], spread[:, 128 * m:128 * (m + 1)], wT[:], start=True, stop=True).then_inc(wb.sem, 1)
                wait(pe, hm, i, MT)
                wait(pe, hw, i, ET)
                pe.wait_ge(down_ld, 32)
                for n in range(NT):
                    wait(pe, ym, i, n - 1 if n >= 2 else 0)
                    for m in range(MT):
                        r = MROWS[m]
                        last = mm(psX[n % 2][:, 0:HID], hid[0:r, m, 128 * n:128 * (n + 1)], wd[0:r, m, :],
                                  start=m == 0, stop=m == MT - 1)
                    last.then_inc(dn.sem, 1)

            with pe.Fori(0, NTF // 2) as t:
                tile(t, 0)
                tile(t, 1)


def kernel(**inputs):
    import numpy as np
    import concourse.bacc as bacc
    from concourse.bass_utils import run_bass_kernel_spmd as run
    a = {k: np.asarray(v) for k, v in inputs.items()}
    n = lambda s: a["L0_attn_" + s]
    f = lambda s: a["L0_ffn_" + s]
    wp = np.stack([n(s).reshape(KT, 128, H, D).transpose(2, 1, 0, 3) for s in ("Wq", "Wk", "Wv", "Wa", "Wg")], 2)
    wp = wp.reshape(H, 128, WCOLS)
    cc = []
    for s in "qkv":
        cc += [n(s + "conv_w").reshape(H, D, TAPS), n(s + "conv_b").reshape(H, D, 1)]
    cc.append(n("ba").reshape(H, D, 1))
    wpack = np.concatenate([wp, *cc], 2)
    wpack = np.concatenate([wpack, np.zeros((2, *wpack.shape[1:]), np.float32)], 0)
    up = f("up_w")
    sg = f("shared_gw")
    wg = np.concatenate([up[:, :HE, :].reshape(E * HE, HID), sg[HS:]], 0).T
    wu = np.concatenate([up[:, HE:, :].reshape(E * HE, HID), sg[:HS]], 0).T
    wd = np.concatenate([f("down_w").transpose(0, 2, 1).reshape(E * HE, HID), f("shared_dw").T], 0)
    arrays = {
        "x": n("x").reshape(T, HID), "wb": n("Wb"), "bb": n("bb"), "wpack": wpack,
        "wo": n("Wo").reshape(H, D, HID).transpose(1, 0, 2), "ln_g": n("ln_g"), "ln_b": n("ln_b"),
        "gate": f("gate_w").T, "gate_bias": f("gate_bias"), "wg": wg, "wu": wu, "wd": wd,
    }
    arrays = {"in_" + k: np.ascontiguousarray(v) for k, v in arrays.items()}
    nc = bacc.Bacc("TRN2", target_bir_lowering=False, num_devices=1)
    args = {k: nc.dram_tensor(k, v.shape, mybir.dt.from_np(v.dtype), kind="ExternalInput").ap()
            for k, v in arrays.items()}
    out = nc.dram_tensor("out", (T, HID), FP32, kind="ExternalOutput").ap()
    build(nc, args, out)
    r = run(nc, [arrays], core_ids=[0])
    return r.results[0]["out"].reshape(1, T, HID)


def build(nc, a, out):
    scr = nc.dram_tensor("scr", (NPROJ, 128, H, T), FP32).ap()
    nbeta = nc.dram_tensor("nbeta", (H, T), FP32).ap()
    att = nc.dram_tensor("att", (T + 2 * C, HID), FP32).ap()
    ctx = ExitStack()
    with ctx:
        ident = ctx.enter_context(nc.sbuf_tensor("ident", [128, 128], FP32))
        made = ctx.enter_context(nc.semaphore("ident_made"))
        with nc.Block() as block:
            @block.gpsimd
            def _(pool):
                nc.gpsimd.memset(ident[:], 0.0).then_inc(made, 1)
                pool.wait_ge(made, 1)
                nc.gpsimd.affine_select(out=ident[:], in_=ident[:], compare_op=ALU.not_equal, fill=1.0, base=0,
                                        pattern=[[-1, 128]], channel_multiplier=1).then_inc(made, 1)
                pool.wait_ge(made, 2)
        project_inputs(nc, ident, a["in_x"], a["in_wb"], a["in_bb"], a["in_wpack"], scr, nbeta)
        recurrence(nc, ident, scr, nbeta, a["in_wo"], a["in_ln_g"], a["in_ln_b"], att)
        feed_forward(nc, ident, a["in_x"], att[2 * C:, :], a["in_gate"], a["in_gate_bias"],
                     a["in_wg"], a["in_wu"], a["in_wd"], out)
```
